# Optimizing a Trainium2 kernel written in Bass

```python
import numpy as np
import jax
import jax.numpy as jnp

def _softmax(x, axis=-1):
    return jax.nn.softmax(x, axis=axis)

def _gelu(x):
    return jax.nn.gelu(x, approximate=True)

def _silu(x):
    return jax.nn.silu(x)

def _sigmoid(x):
    return jax.nn.sigmoid(x)

def _layernorm(x, axis=-1, eps=1e-05):
    m = jnp.mean(x, axis=axis, keepdims=True)
    v = jnp.var(x, axis=axis, keepdims=True)
    return (x - m) / jnp.sqrt(v + eps)

def _scatter_add(tgt, idx, src, axis=0):
    return tgt.at[idx].add(src)

def _segment_sum(src, seg, n):
    return jax.ops.segment_sum(src, seg, n)
kernel_name = 'mk_gnn_resnorm_d4_gnn_r32_8fe7c4'

def setup_inputs(seed: int=0):
    np.random.seed(seed)
    _w = jnp.asarray

    def _rec_inputs():
        import jax
        import jax.numpy as jnp
        _gk = jax.random.key(seed)
        x = -0.001003 + 1 * jax.random.normal(jax.random.fold_in(_gk, 1), (64, 768), jnp.float32)
        _s = jax.random.randint(jax.random.fold_in(_gk, 2), (1024,), 0, 64, jnp.int32)
        _d = jax.random.randint(jax.random.fold_in(_gk, 3), (1024,), 0, 64, jnp.int32)
        _loop = jnp.arange(64, dtype=jnp.int32)
        src = jnp.concatenate([_s, _d, _loop])
        dst = jnp.concatenate([_d, _s, _loop])
        _o = jnp.argsort(dst, stable=True)
        src = src[_o]
        dst = dst[_o]
        edge_type_3 = jax.random.randint(jax.random.fold_in(_gk, 12), (2112,), 0, 3, jnp.int32)
        edge_type_8 = jax.random.randint(jax.random.fold_in(_gk, 13), (2112,), 0, 8, jnp.int32)
        return (x, src, dst, edge_type_3, edge_type_8)
    x, src, dst, edge_type_3, edge_type_8 = _rec_inputs()

    def _L0_gnn_setup():
        import jax, jax.numpy as jnp
        import numpy as np
        NUM_RELATIONS = 3

        def _rgcn(x, W_rel, W_root, bias, src, dst, etype):
            n = x.shape[0]
            xr = jnp.einsum('ni,rio->rno', x, W_rel)
            msg = xr[etype, src]
            out = x @ W_root + bias
            for r in range(NUM_RELATIONS):
                m = etype == r
                s = jax.ops.segment_sum(jnp.where(m[:, None], msg, 0.0), dst, num_segments=n)
                c = jax.ops.segment_sum(m.astype(x.dtype), dst, num_segments=n)
                out = out + s / jnp.maximum(c, 1.0)[:, None]
            return out

        def _gate(h, q, Wg, bg, Wq, bq):
            B, L, F = q.shape
            N = h.shape[0] // B
            h3 = h.reshape(B, N, F)
            hg = jnp.einsum('bnf,gf->bng', h3, Wg[:, :F])
            qg = jnp.einsum('blf,gf->blg', q, Wg[:, F:]) + bg
            attn = jax.nn.sigmoid(hg[:, :, None, :] + qg[:, None, :, :])
            qi = jnp.einsum('bnlf,blf->bnf', attn, q)
            alpha = jax.nn.sigmoid(jnp.einsum('bnf,gf->bng', h3, Wq[:, :F]) + jnp.einsum('bnf,gf->bng', qi, Wq[:, F:]) + bq)
            hn = alpha * jnp.tanh(qi) + (1.0 - alpha) * h3
            return hn.reshape(B * N, F)
        key = jax.random.key(seed)
        ks = jax.random.split(key, 16)
        F = 768
        BN, E, B, L = (64, 2048, 8, 64)
        s = 0.02
        return {'x': jax.random.normal(ks[0], (BN, F), jnp.float32), 'edge_index': jax.random.randint(ks[1], (2, E), 0, BN), 'edge_type': jax.random.randint(ks[2], (E,), 0, NUM_RELATIONS), 'query_embs': jax.random.normal(ks[3], (B, L, F), jnp.float32), 'W_rel1': jax.random.normal(ks[4], (NUM_RELATIONS, F, F), jnp.float32) * s, 'W_root1': jax.random.normal(ks[5], (F, F), jnp.float32) * s, 'b1': jnp.zeros((F,), jnp.float32), 'W_rel2': jax.random.normal(ks[6], (NUM_RELATIONS, F, F), jnp.float32) * s, 'W_root2': jax.random.normal(ks[7], (F, F), jnp.float32) * s, 'b2': jnp.zeros((F,), jnp.float32), 'Wg': jax.random.normal(ks[8], (F, 2 * F), jnp.float32) * s, 'bg': jnp.zeros((F,), jnp.float32), 'Wq': jax.random.normal(ks[9], (F, 2 * F), jnp.float32) * s, 'bq': jnp.zeros((F,), jnp.float32)}
    _L0_gnn_all = _L0_gnn_setup()
    _L0_gnn_in = {k: v for k, v in _L0_gnn_all.items() if k in ('query_embs', 'W_rel1', 'W_root1', 'b1', 'W_rel2', 'W_root2', 'b2', 'Wg', 'bg', 'Wq', 'bq')}
    del _L0_gnn_all

    def _L1_gnn_setup():
        import jax, jax.numpy as jnp
        import numpy as np
        N_NODES = 10000
        D = 768
        N_EDGES = 5000

        def gcn_conv(x, W, b, src, dst, n_nodes):
            h = x @ W
            deg = jax.ops.segment_sum(jnp.ones_like(dst, dtype=h.dtype), dst, num_segments=n_nodes)
            dinv = jnp.where(deg > 0, jax.lax.rsqrt(deg), 0.0)
            norm = dinv[src] * dinv[dst]
            msgs = h[src] * norm[:, None]
            out = jax.ops.segment_sum(msgs, dst, num_segments=n_nodes)
            return out + b

        def add_self_loops(edge_index, n_nodes):
            loop = jnp.arange(n_nodes, dtype=edge_index.dtype)
            src = jnp.concatenate([edge_index[0], loop])
            dst = jnp.concatenate([edge_index[1], loop])
            return (src, dst)
        key = jax.random.key(seed)
        k1, k2, k3, k4 = jax.random.split(key, 4)
        x = jax.random.normal(k1, (N_NODES, D), dtype=jnp.float32)
        edge_index = jax.random.randint(k2, (2, N_EDGES), 0, N_NODES, dtype=jnp.int32)
        glorot = float(np.sqrt(6.0 / (D + D)))
        W1 = jax.random.uniform(k3, (D, D), jnp.float32, -glorot, glorot)
        W2 = jax.random.uniform(k4, (D, D), jnp.float32, -glorot, glorot)
        b1 = jnp.zeros((D,), jnp.float32)
        b2 = jnp.zeros((D,), jnp.float32)
        return {'x': x, 'W1': W1, 'b1': b1, 'W2': W2, 'b2': b2, 'edge_index': edge_index}
    _L1_gnn_all = _L1_gnn_setup()
    _L1_gnn_in = {k: v for k, v in _L1_gnn_all.items() if k in ('W1', 'b1', 'W2', 'b2')}
    del _L1_gnn_all

    def _L2_gnn_setup():
        import jax, jax.numpy as jnp
        import numpy as np
        N_NODES = 10000
        N_EDGES = 3125
        DIM = 768
        NEG_SLOPE = 0.2

        def gat_conv(x, src, dst, W, att_src, att_dst, bias, num_nodes):
            h = x @ W
            a_s = h @ att_src
            a_d = h @ att_dst
            e = jax.nn.leaky_relu(a_s[src] + a_d[dst], NEG_SLOPE)
            m = jax.ops.segment_max(e, dst, num_segments=num_nodes)
            e = jnp.exp(e - m[dst])
            denom = jax.ops.segment_sum(e, dst, num_segments=num_nodes)
            alpha = e / denom[dst]
            msg = alpha[:, None] * h[src]
            out = jax.ops.segment_sum(msg, dst, num_segments=num_nodes)
            return out + bias
        key = jax.random.key(seed)
        ks = jax.random.split(key, 12)
        s = 1.0 / np.sqrt(DIM)
        inp = {'x': jax.random.normal(ks[0], (N_NODES, DIM), dtype=jnp.float32), 'edge_index': jax.random.randint(ks[1], (2, N_EDGES), 0, N_NODES, dtype=jnp.int64), 'W1': jax.random.normal(ks[2], (DIM, DIM), dtype=jnp.float32) * s, 'att_src1': jax.random.normal(ks[3], (DIM,), dtype=jnp.float32) * s, 'att_dst1': jax.random.normal(ks[4], (DIM,), dtype=jnp.float32) * s, 'b1': jnp.zeros((DIM,), dtype=jnp.float32), 'W2': jax.random.normal(ks[5], (DIM, DIM), dtype=jnp.float32) * s, 'att_src2': jax.random.normal(ks[6], (DIM,), dtype=jnp.float32) * s, 'att_dst2': jax.random.normal(ks[7], (DIM,), dtype=jnp.float32) * s, 'b2': jnp.zeros((DIM,), dtype=jnp.float32)}
        return inp
    _L2_gnn_all = _L2_gnn_setup()
    _L2_gnn_in = {k: v for k, v in _L2_gnn_all.items() if k in ('W1', 'att_src1', 'att_dst1', 'b1', 'W2', 'att_src2', 'att_dst2', 'b2')}
    del _L2_gnn_all

    def _L3_gnn_setup():
        import jax, jax.numpy as jnp
        import numpy as np
        N, IN, OUT, R, E = (625, 768, 768, 8, 10000)

        def _rgcn_conv(x, src, dst, etype, W, root, b):
            num_nodes = x.shape[0]
            num_rel = W.shape[0]
            x_src = x[src]
            seg = dst * num_rel + etype
            sums = jax.ops.segment_sum(x_src, seg, num_segments=num_nodes * num_rel)
            cnt = jax.ops.segment_sum(jnp.ones((src.shape[0],), dtype=x.dtype), seg, num_segments=num_nodes * num_rel)
            mean = sums / jnp.maximum(cnt, 1.0)[:, None]
            mean = mean.reshape(num_nodes, num_rel, -1)
            out = jnp.einsum('nri,rio->no', mean, W)
            return out + x @ root + b
        key = jax.random.key(seed)
        ks = jax.random.split(key, 9)
        x = jax.random.normal(ks[0], (N, IN), dtype=jnp.float32)
        edge_index = jax.random.randint(ks[1], (2, E), 0, N, dtype=jnp.int64)
        edge_type = jax.random.randint(ks[2], (E,), 0, R, dtype=jnp.int64)
        s1 = 1.0 / np.sqrt(IN)
        s2 = 1.0 / np.sqrt(OUT)
        W1 = jax.random.normal(ks[3], (R, IN, OUT), dtype=jnp.float32) * s1
        root1 = jax.random.normal(ks[4], (IN, OUT), dtype=jnp.float32) * s1
        b1 = jnp.zeros((OUT,), dtype=jnp.float32)
        W2 = jax.random.normal(ks[5], (R, OUT, OUT), dtype=jnp.float32) * s2
        root2 = jax.random.normal(ks[6], (OUT, OUT), dtype=jnp.float32) * s2
        b2 = jnp.zeros((OUT,), dtype=jnp.float32)
        return {'x': x, 'edge_index': edge_index, 'edge_type': edge_type, 'W1': W1, 'root1': root1, 'b1': b1, 'W2': W2, 'root2': root2, 'b2': b2}
    _L3_gnn_all = _L3_gnn_setup()
    _L3_gnn_in = {k: v for k, v in _L3_gnn_all.items() if k in ('W1', 'root1', 'b1', 'W2', 'root2', 'b2')}
    del _L3_gnn_all
    return {'x': x, 'src': src, 'dst': dst, 'edge_type_3': edge_type_3, 'edge_type_8': edge_type_8, 'L0_gnn_query_embs': _L0_gnn_in['query_embs'], 'L0_gnn_W_rel1': _L0_gnn_in['W_rel1'], 'L0_gnn_W_root1': _L0_gnn_in['W_root1'], 'L0_gnn_b1': _L0_gnn_in['b1'], 'L0_gnn_W_rel2': _L0_gnn_in['W_rel2'], 'L0_gnn_W_root2': _L0_gnn_in['W_root2'], 'L0_gnn_b2': _L0_gnn_in['b2'], 'L0_gnn_Wg': _L0_gnn_in['Wg'], 'L0_gnn_bg': _L0_gnn_in['bg'], 'L0_gnn_Wq': _L0_gnn_in['Wq'], 'L0_gnn_bq': _L0_gnn_in['bq'], 'L1_gnn_W1': _L1_gnn_in['W1'], 'L1_gnn_b1': _L1_gnn_in['b1'], 'L1_gnn_W2': _L1_gnn_in['W2'], 'L1_gnn_b2': _L1_gnn_in['b2'], 'L2_gnn_W1': _L2_gnn_in['W1'], 'L2_gnn_att_src1': _L2_gnn_in['att_src1'], 'L2_gnn_att_dst1': _L2_gnn_in['att_dst1'], 'L2_gnn_b1': _L2_gnn_in['b1'], 'L2_gnn_W2': _L2_gnn_in['W2'], 'L2_gnn_att_src2': _L2_gnn_in['att_src2'], 'L2_gnn_att_dst2': _L2_gnn_in['att_dst2'], 'L2_gnn_b2': _L2_gnn_in['b2'], 'L3_gnn_W1': _L3_gnn_in['W1'], 'L3_gnn_root1': _L3_gnn_in['root1'], 'L3_gnn_b1': _L3_gnn_in['b1'], 'L3_gnn_W2': _L3_gnn_in['W2'], 'L3_gnn_root2': _L3_gnn_in['root2'], 'L3_gnn_b2': _L3_gnn_in['b2']}

def reference(x, src, dst, edge_type_3, edge_type_8, L0_gnn_query_embs, L0_gnn_W_rel1, L0_gnn_W_root1, L0_gnn_b1, L0_gnn_W_rel2, L0_gnn_W_root2, L0_gnn_b2, L0_gnn_Wg, L0_gnn_bg, L0_gnn_Wq, L0_gnn_bq, L1_gnn_W1, L1_gnn_b1, L1_gnn_W2, L1_gnn_b2, L2_gnn_W1, L2_gnn_att_src1, L2_gnn_att_dst1, L2_gnn_b1, L2_gnn_W2, L2_gnn_att_src2, L2_gnn_att_dst2, L2_gnn_b2, L3_gnn_W1, L3_gnn_root1, L3_gnn_b1, L3_gnn_W2, L3_gnn_root2, L3_gnn_b2):
    import jax
    import jax.numpy as jnp

    def _L0_gnn_ref(x, edge_index, edge_type, query_embs, W_rel1, W_root1, b1, W_rel2, W_root2, b2, Wg, bg, Wq, bq):
        import jax, jax.numpy as jnp
        import numpy as np
        NUM_RELATIONS = 3

        def _rgcn(x, W_rel, W_root, bias, src, dst, etype):
            n = x.shape[0]
            xr = jnp.einsum('ni,rio->rno', x, W_rel)
            msg = xr[etype, src]
            out = x @ W_root + bias
            for r in range(NUM_RELATIONS):
                m = etype == r
                s = jax.ops.segment_sum(jnp.where(m[:, None], msg, 0.0), dst, num_segments=n)
                c = jax.ops.segment_sum(m.astype(x.dtype), dst, num_segments=n)
                out = out + s / jnp.maximum(c, 1.0)[:, None]
            return out

        def _gate(h, q, Wg, bg, Wq, bq):
            B, L, F = q.shape
            N = h.shape[0] // B
            h3 = h.reshape(B, N, F)
            hg = jnp.einsum('bnf,gf->bng', h3, Wg[:, :F])
            qg = jnp.einsum('blf,gf->blg', q, Wg[:, F:]) + bg
            attn = jax.nn.sigmoid(hg[:, :, None, :] + qg[:, None, :, :])
            qi = jnp.einsum('bnlf,blf->bnf', attn, q)
            alpha = jax.nn.sigmoid(jnp.einsum('bnf,gf->bng', h3, Wq[:, :F]) + jnp.einsum('bnf,gf->bng', qi, Wq[:, F:]) + bq)
            hn = alpha * jnp.tanh(qi) + (1.0 - alpha) * h3
            return hn.reshape(B * N, F)
        src, dst = (edge_index[0], edge_index[1])
        h = jax.nn.relu(_rgcn(x, W_rel1, W_root1, b1, src, dst, edge_type))
        h = _gate(h, query_embs, Wg, bg, Wq, bq)
        h = jax.nn.relu(_rgcn(h, W_rel2, W_root2, b2, src, dst, edge_type))
        h = _gate(h, query_embs, Wg, bg, Wq, bq)
        return h

    def _L1_gnn_ref(x, W1, b1, W2, b2, edge_index):
        import jax, jax.numpy as jnp
        import numpy as np
        N_NODES = 10000
        D = 768
        N_EDGES = 5000

        def gcn_conv(x, W, b, src, dst, n_nodes):
            h = x @ W
            deg = jax.ops.segment_sum(jnp.ones_like(dst, dtype=h.dtype), dst, num_segments=n_nodes)
            dinv = jnp.where(deg > 0, jax.lax.rsqrt(deg), 0.0)
            norm = dinv[src] * dinv[dst]
            msgs = h[src] * norm[:, None]
            out = jax.ops.segment_sum(msgs, dst, num_segments=n_nodes)
            return out + b

        def add_self_loops(edge_index, n_nodes):
            loop = jnp.arange(n_nodes, dtype=edge_index.dtype)
            src = jnp.concatenate([edge_index[0], loop])
            dst = jnp.concatenate([edge_index[1], loop])
            return (src, dst)
        n = x.shape[0]
        src, dst = add_self_loops(edge_index, n)
        h = gcn_conv(x, W1, b1, src, dst, n)
        h = jax.nn.relu(h)
        out = gcn_conv(h, W2, b2, src, dst, n)
        return out

    def _L2_gnn_ref(x, edge_index, W1, att_src1, att_dst1, b1, W2, att_src2, att_dst2, b2):
        import jax, jax.numpy as jnp
        import numpy as np
        N_NODES = 10000
        N_EDGES = 3125
        DIM = 768
        NEG_SLOPE = 0.2

        def gat_conv(x, src, dst, W, att_src, att_dst, bias, num_nodes):
            h = x @ W
            a_s = h @ att_src
            a_d = h @ att_dst
            e = jax.nn.leaky_relu(a_s[src] + a_d[dst], NEG_SLOPE)
            m = jax.ops.segment_max(e, dst, num_segments=num_nodes)
            e = jnp.exp(e - m[dst])
            denom = jax.ops.segment_sum(e, dst, num_segments=num_nodes)
            alpha = e / denom[dst]
            msg = alpha[:, None] * h[src]
            out = jax.ops.segment_sum(msg, dst, num_segments=num_nodes)
            return out + bias
        n = x.shape[0]
        loops = jnp.arange(n, dtype=edge_index.dtype)
        src = jnp.concatenate([edge_index[0], loops])
        dst = jnp.concatenate([edge_index[1], loops])
        h = gat_conv(x, src, dst, W1, att_src1, att_dst1, b1, n)
        h = jax.nn.relu(h)
        out = gat_conv(h, src, dst, W2, att_src2, att_dst2, b2, n)
        return out

    def _L3_gnn_ref(x, edge_index, edge_type, W1, root1, b1, W2, root2, b2):
        import jax, jax.numpy as jnp
        import numpy as np
        N, IN, OUT, R, E = (625, 768, 768, 8, 10000)

        def _rgcn_conv(x, src, dst, etype, W, root, b):
            num_nodes = x.shape[0]
            num_rel = W.shape[0]
            x_src = x[src]
            seg = dst * num_rel + etype
            sums = jax.ops.segment_sum(x_src, seg, num_segments=num_nodes * num_rel)
            cnt = jax.ops.segment_sum(jnp.ones((src.shape[0],), dtype=x.dtype), seg, num_segments=num_nodes * num_rel)
            mean = sums / jnp.maximum(cnt, 1.0)[:, None]
            mean = mean.reshape(num_nodes, num_rel, -1)
            out = jnp.einsum('nri,rio->no', mean, W)
            return out + x @ root + b
        src, dst = (edge_index[0], edge_index[1])
        h = _rgcn_conv(x, src, dst, edge_type, W1, root1, b1)
        h = jax.nn.relu(h)
        out = _rgcn_conv(h, src, dst, edge_type, W2, root2, b2)
        return out
    edge_index = jnp.stack([src, dst])
    x = _layernorm(x + _L0_gnn_ref(x, edge_index, edge_type_3, L0_gnn_query_embs, L0_gnn_W_rel1, L0_gnn_W_root1, L0_gnn_b1, L0_gnn_W_rel2, L0_gnn_W_root2, L0_gnn_b2, L0_gnn_Wg, L0_gnn_bg, L0_gnn_Wq, L0_gnn_bq), axis=-1)
    x = _layernorm(x + _L1_gnn_ref(x, L1_gnn_W1, L1_gnn_b1, L1_gnn_W2, L1_gnn_b2, edge_index), axis=-1)
    x = _layernorm(x + _L2_gnn_ref(x, edge_index, L2_gnn_W1, L2_gnn_att_src1, L2_gnn_att_dst1, L2_gnn_b1, L2_gnn_W2, L2_gnn_att_src2, L2_gnn_att_dst2, L2_gnn_b2), axis=-1)
    x = _layernorm(x + _L3_gnn_ref(x, edge_index, edge_type_8, L3_gnn_W1, L3_gnn_root1, L3_gnn_b1, L3_gnn_W2, L3_gnn_root2, L3_gnn_b2), axis=-1)
    return x

_drawn_inputs = setup_inputs


def setup_inputs(seed=0):
    import zlib

    import numpy as np

    out = dict(_drawn_inputs(seed))
    spreads = {'L0_gnn_b1': (0.0, 0.497),
     'L0_gnn_b2': (0.0, 0.1),
     'L0_gnn_bg': (0.0, 0.468),
     'L0_gnn_bq': (0.0, 0.554),
     'L1_gnn_b1': (0.0, 0.1),
     'L1_gnn_b2': (0.0, 0.1),
     'L2_gnn_b1': (0.0, 0.1),
     'L2_gnn_b2': (0.0, 0.1),
     'L3_gnn_b1': (0.0, 0.1),
     'L3_gnn_b2': (0.0, 0.301)}
    factors = {'L2_gnn_att_dst1': 78.893, 'L2_gnn_att_src2': 26.8, 'L2_gnn_att_dst2': 200.0}
    for name, (base, spread) in spreads.items():
        noise = np.random.default_rng([zlib.crc32(name.encode()), seed]).standard_normal(out[name].shape)
        drawn = base * np.exp(spread * noise) if base else spread * noise
        out[name] = jnp.asarray(drawn.astype(out[name].dtype))
    for name, factor in factors.items():
        out[name] = (out[name] * factor).astype(out[name].dtype)
    return out
```

```python
from contextlib import ExitStack

import concourse.bass as bass
import numpy as np
from concourse import mybir

F32 = mybir.dt.float32
BF16 = mybir.dt.bfloat16
I32 = mybir.dt.int32
ALU = mybir.AluOpType
ACT = mybir.ActivationFunctionType
AX = mybir.AxisListType

P = 128
N = 64
D = 768
HD = D // 2
KC = D // P
E = 2112
EP = 96
ET = E // EP
B, L = 8, 64
NB = N // B
TILES = N // 2
EPS = 1e-5
SLOPE = 0.2
R3, R8 = 3, 8
MAT = KC * D
FAR = 1e30

NAMES = (["rel1_0", "rel1_1", "rel1_2", "root1", "rel2_0", "rel2_1", "rel2_2", "root2",
          "Wg_h", "Wg_q", "Wq_h", "Wq_q", "gcn1", "gcn2", "gat1", "gat2"]
         + [f"r8a_{r}" for r in range(R8)] + ["r8a_root"] + [f"r8b_{r}" for r in range(R8)] + ["r8b_root"])
LOADS = (["Q", "Wg_q", "root1", "rel1_0", "rel1_1", "rel1_2", "Wg_h", "Wq_h", "Wq_q",
          "root2", "rel2_0", "rel2_1", "rel2_2", "Wg_h", "Wq_h", "Wq_q", "gcn1", "gcn2", "gat1", "gat2",
          "r8a_root"] + [f"r8a_{r}" for r in range(R8)] + ["r8b_root"] + [f"r8b_{r}" for r in range(R8)])
FIRST_SLOTS = 4
ALL_SLOTS = 8
WIDE_FROM = LOADS.index("gat1")

BIAS = ["L0_b1", "L0_b2", "L0_bq", "L1_b1", "L1_b2", "L2_b1", "L2_b2", "L3_b1", "L3_b2", "L0_bg"]
BG = len(BIAS) - 1

C_EYE = 0
C_SUM = C_EYE + N
C_AVG = C_SUM + 2 * N - 2
C_DIF = C_AVG + P
C_PAIR = C_DIF + P
C_ONE = C_PAIR + P
C_BIAS = C_ONE + P
C_IOTA = C_BIAS + (len(BIAS) + 1) * N
C_END = C_IOTA + R8 * N


def constants():
    c = np.zeros((P, C_END), np.float32)
    p = np.arange(P)
    same = (p[:, None] % N == p[None, :] % N).astype(np.float32)
    c[:, C_EYE:C_EYE + N] = same[:, :N]
    c[:N, C_SUM + N - 2] = 1
    c[N:, C_SUM + N - 1] = 1
    c[:, C_AVG:C_AVG + P] = same / 2
    c[:, C_DIF:C_DIF + P] = np.eye(P, dtype=np.float32) - same / 2
    c[:, C_PAIR:C_PAIR + P] = same
    c[:, C_ONE:C_ONE + P] = 1
    for i in range(len(BIAS)):
        c[i, C_BIAS + i * N:C_BIAS + (i + 1 + (i == BG)) * N] = 1
    c[:, C_IOTA:C_END] = np.arange(R8 * N)
    return c


def ring():
    slots, held, uses, out = [], {}, {}, []
    for i in range(len(LOADS)):
        if i < WIDE_FROM:
            s = i % FIRST_SLOTS
        elif i < WIDE_FROM + FIRST_SLOTS:
            s = FIRST_SLOTS + i - WIDE_FROM
        elif i < WIDE_FROM + ALL_SLOTS:
            s = slots[i - ALL_SLOTS]
        else:
            s = slots[i - ALL_SLOTS]
        slots.append(s)
        uses[s] = uses.get(s, 0) + 1
        out.append((s, uses[s], held.get(s)))
        held[s] = i
    return out


RING = ring()
CONVS = ["rgcn1", "rgcn2", "gcn1", "gcn2", "gat1", "gat2", "r8a", "r8b"]


def build(nc, x, edges, consts, biases, query_t, query, att, weights, out):
    with ExitStack() as ctx:
        def sb(name, shape, dt=F32):
            return ctx.enter_context(nc.sbuf_tensor(name, shape, dt))

        def sem(name):
            return ctx.enter_context(nc.semaphore(name))

        def sems(what, names):
            return {n: sem(f"{what}_{n}") for n in names}

        ps_t = ctx.enter_context(nc.psum_tensor("ps_t", [P, 2, 512], F32))
        ps_x = ctx.enter_context(nc.psum_tensor("ps_x", [P, 512], F32))
        ps_acc = ctx.enter_context(nc.psum_tensor("ps_acc", [P, 512], F32))
        ps_g = ctx.enter_context(nc.psum_tensor("ps_g", [P, 4, 512], F32))
        ps_qi = ps_t[:, 0, 0:HD]
        ps_s = ps_t[:, 1, :]
        acc = ps_acc[:, 0:HD]
        xt_ps = [ps_x[:, 0:3 * N], ps_t[:, 1, 0:3 * N]]

        w_ring = sb("w_ring", [P, FIRST_SLOTS, MAT])
        gatebuf = sb("gatebuf", [P, ALL_SLOTS - FIRST_SLOTS, MAT])
        flat = gatebuf[:, :, :].rearrange("p a b -> p (a b)")
        third = flat.shape[1] // 3
        q_rows = flat[:, 0:third].rearrange("p (b f) -> p b f", b=B)
        qparts = flat[:, third:2 * third].bitcast(BF16)
        qg_hm = qparts[:, 0:B * D].rearrange("p (b f) -> p b f", b=B)
        lows = qparts[:, B * D:2 * B * D].rearrange("p (b h f) -> p b h f", b=B, h=2)
        sel = flat[:, 2 * third:].bitcast(BF16).rearrange("p (k c) -> p k c", k=3)
        sel_node, sel_low = sel[:, 0, :], [sel[:, 1, :], sel[:, 2, :]]
        work = sb("work", [P, 6144])
        mt = work[:, 0:KC * 512]
        att_s = work[:, 3072:3072 + 2 * D].rearrange("p (t f) -> p t f", t=2)
        prod = work[:, 3072 + 2 * D:3072 + 4 * D].rearrange("p (t f) -> p t f", t=2)
        hot8 = work[:, 0:ET * R8 * N // 2].bitcast(BF16).rearrange("p (t k) -> p t k", t=ET)
        hot3 = flat[:, 2 * third:2 * third + ET * R3 * N // 2].bitcast(BF16).rearrange("p (t k) -> p t k", t=ET)
        att_rows = sb("att_rows", [P, 4, HD])
        hot_src = att_rows[:, :, :].rearrange("p a b -> p (a b)")[:, 0:ET * P // 2].bitcast(BF16).rearrange("p (t k) -> p t k", t=ET)
        cst = sb("cst", [P, C_END])
        bias_rows = sb("bias_rows", [len(BIAS), D])
        edges_i = sb("edges_i", [EP, 4, ET], I32)
        edges_f = sb("edges_f", [EP, 4, ET])
        keys = sb("keys", [EP, 2, ET])
        a3 = sb("a3", [P, R3 * N])
        a8 = sb("a8", [P, R8 * N])
        cnt8 = work[:, ET * R8 * N // 2:ET * R8 * N // 2 + R8 * N]
        c_sd = sb("c_sd", [P, 2, N])
        c_ds = sb("c_ds", [P, N])
        far = sb("far", [P, N])
        mask = sb("mask", [P, N])
        dinv_row = sb("dinv_row", [P, N])
        dinv_col = sb("dinv_col", [P, 1])
        deg = sb("deg", [P, 1])
        ahat = sb("ahat", [P, N])
        eye_b = sb("eye_b", [P, P], BF16)
        xs = {n: sb(f"x_{n}", [P, HD]) for n in ("in", "a", "b", "y")}
        cnt3 = xs["b"][:, 0:R3 * N]
        x_low = sb("x_low", [P, HD])
        mid = sb("mid", [P, HD], BF16)
        low = sb("low", [P, HD], BF16)
        hg_hm = sb("hg_hm", [P, 2, HD], BF16)
        th = x_low
        qi = sb("qi", [P, HD])
        alpha = xs["b"]
        xt = sb("xt", [P, KC * N])
        qit = sb("qit", [P, KC * N])
        stat = sb("stat", [P, 6])
        mv = sb("mv", [P, 2])
        st = sb("st", [P, 8])
        a_part = sb("a_part", [P, 2])
        diag = sb("diag", [P, N])
        e_t = sb("e_t", [P, 5, N])
        al_t = sb("al_t", [P, 2, N])
        power = sb("power", [P, N])
        table = sb("table", [P, 1])

        eye, one = cst[:, C_EYE:C_EYE + N], cst[:, C_ONE:C_ONE + P]
        iota = cst[0:EP, C_IOTA:C_END]

        def bias_pick(i):
            return cst[0:len(BIAS), C_BIAS + i * N:C_BIAS + (i + 1) * N]

        def last_of(name):
            first = {"rgcn1": 2, "hg_g1": 6, "al_g1": 8, "rgcn2": 9, "hg_g2": 13, "al_g2": 15, "gcn1": 16, "gcn2": 17,
                     "gat1": 18, "gat2": 19, "r8a": 20, "r8b": 20 + R8 + 1}[name]
            return first + 1 + (R3 if name.startswith("rgcn") else R8 if name.startswith("r8") else 0)

        def slot(i):
            s = RING[i][0]
            return w_ring[:, s, :] if s < FIRST_SLOTS else gatebuf[:, s - FIRST_SLOTS, :]

        const_in, edges_in, x_in, bias_in, att_in = (sem(n) for n in ("const_in", "edges_in", "x_in", "bias_in", "att_in"))
        query_in, out_done = sem("query_in"), sem("out_done")
        loaded = [sem(f"loaded_{s}") for s in range(ALL_SLOTS)]
        used = sem("weights_used")
        vec = sem("vec_chain")
        hot3_ready, hot8_ready = sem("hot3_ready"), sem("hot8_ready")
        counts3, counts8 = sem("counts3"), sem("counts8")
        a3_copied, a8_copied = sem("a3_copied"), sem("a8_copied")
        cnt3_ps, cnt8_ps, a3_ready, a8_ready = (sem(n) for n in ("cnt3_ps", "cnt8_ps", "a3_ready", "a8_ready"))
        csd_ready, cds_ps, deg_ready = sem("csd_ready"), sem("cds_ps"), sem("deg_ready")
        qg_ps, qg_copied_v, qg_copied_a = sem("qg_ps"), sem("qg_copied_v"), sem("qg_copied_a")
        sel_ready = sem("sel_ready")
        state = sems("state", CONVS)
        xt_done = sems("xt_done", CONVS)
        xt_copied = sems("xt_copied", CONVS)
        mt_done = {n: [sem(f"mt_done_{n}_{h}") for h in range(2)] for n in ("rgcn1", "rgcn2", "r8a", "r8b")}
        mt_v = sems("mt_v", ["rgcn1", "rgcn2", "r8a", "r8b"])
        mt_a = sems("mt_a", ["rgcn1", "rgcn2", "r8a", "r8b"])
        gates = ["g1", "g2"]
        h_ready, ht_done, ht_copied, hg_split = (sems(n, gates) for n in ("h_ready", "ht_done", "ht_copied", "hg_split"))
        tile_sum, tile_sig, tile_prod, tile_red = (sems(n, gates) for n in ("tile_sum", "tile_sig", "tile_prod", "tile_red"))
        qi_copied, tanh_done, qit_done, qit_copied, al_done = (
            sems(n, gates) for n in ("qi_copied", "tanh_done", "qit_done", "qit_copied", "al_done"))
        norms = ["n0", "n1", "n2", "n3"]
        mv_ready, mv_ps, var_ready, rstd_ready = (sems(n, norms) for n in ("mv_ready", "mv_ps", "var_ready", "rstd_ready"))
        dinv_ready, power_set = sem("dinv_ready"), sem("power_set")
        gats = ["gat1", "gat2"]
        parts_ready, logits_ps, exp_in, exp_done, alpha_ready, alphat_ps, alphat_ready, mix_done = (
            sems(n, gats) for n in ("parts_ready", "logits_ps", "exp_in", "exp_done", "alpha_ready", "alphat_ps", "alphat_ready", "mix_done"))
        result = sem("result")

        block = ctx.enter_context(nc.Block())

        @block.sync
        def _(sp):
            sp.dma_start(edges_i[:, :, :], edges).then_inc(edges_in, 16)
            sp.dma_start(cst[:, :], consts).then_inc(const_in, 16)
            for h in range(2):
                sp.dma_start(xs["in"][h * N:(h + 1) * N, :], x[:, h * HD:(h + 1) * HD]).then_inc(x_in, 16)
            sp.dma_start(bias_rows[:, :], biases).then_inc(bias_in, 16)
            for i, name in enumerate(LOADS):
                s, _, before = RING[i]
                if before is not None:
                    sp.wait_ge(used, before + 1)
                if i == WIDE_FROM:
                    sp.wait_ge(tile_red["g2"], TILES)
                if name == "Q":
                    sp.dma_start(slot(i)[:, 0:KC * B * L], query_t).then_inc(loaded[s], 16)
                else:
                    sp.dma_start(slot(i), weights[NAMES.index(name)]).then_inc(loaded[s], 16)
                if i == FIRST_SLOTS:
                    for h in range(2):
                        sp.dma_start(q_rows[h * N:(h + 1) * N, :, :], query).then_inc(query_in, 16)
                    sp.wait_ge(counts8, 1)
                    for k in range(4):
                        for h in range(2):
                            sp.dma_start(att_rows[h * N:(h + 1) * N, k, :],
                                         att[k:k + 1, h * HD:(h + 1) * HD].to_broadcast([N, HD])).then_inc(att_in, 16)
            sp.wait_ge(result, 1)
            for h in range(2):
                sp.dma_start(out[:, h * HD:(h + 1) * HD], xs["y"][h * N:(h + 1) * N, :]).then_inc(out_done, 16)
            sp.wait_ge(out_done, 32)

        @block.gpsimd
        def _(pool):
            nc.gpsimd.memset(power[:, :], -0.5).then_inc(power_set, 1)
            pool.wait_ge(power_set, 1)
            pool.wait_ge(const_in, 16)
            pool.wait_ge(deg_ready, 1)
            nc.gpsimd.tensor_tensor(dinv_col[:, :], deg[:, :], power[:, 0:1], ALU.pow).then_inc(dinv_ready, 1)
            pool.wait_ge(dinv_ready, 1)
            nc.gpsimd.tensor_tensor(dinv_row[:, :], dinv_row[:, :], power[:, :], ALU.pow).then_inc(dinv_ready, 1)
            pool.wait_ge(dinv_ready, 2)
            for i, (k, rows) in enumerate(((0, (0, P)), (1, (0, N)), (2, (N, P)))):
                a, b = rows
                if i:
                    pool.wait_ge(sel_ready, i)
                nc.gpsimd.tensor_copy(sel[a:b, k, :].rearrange("p (n l) -> p n l", l=L),
                                      eye[a:b, :].unsqueeze(2).to_broadcast([b - a, N, L])).then_inc(sel_ready, 1)
            for i, (k, rows) in enumerate(((1, (N, P)), (2, (0, N)))):
                a, b = rows
                pool.wait_ge(sel_ready, 3 + i)
                nc.gpsimd.tensor_copy(sel[a:b, k, :].rearrange("p (n l) -> p n l", l=L),
                                      eye[a:b, :].unsqueeze(1).to_broadcast([b - a, N, L])).then_inc(sel_ready, 1)
            pool.wait_ge(sel_ready, 5)
            for n in norms:
                pool.wait_ge(var_ready[n], 1)
                nc.gpsimd.tensor_tensor(st[:, 4:5], st[:, 3:4], power[:, 0:1], ALU.pow).then_inc(rstd_ready[n], 1)

        @block.tensor
        def _(pe):
            mm = nc.tensor.matmul

            def weights_of(i):
                pe.wait_ge(loaded[RING[i][0]], 16 * RING[i][1])
                return slot(i).rearrange("p (c n) -> p c n", c=KC)

            def bias(name):
                i = BIAS.index(name)
                for h in range(2):
                    mm(acc[h * N:(h + 1) * N, :], bias_pick(i), bias_rows[:, h * HD:(h + 1) * HD],
                       start=True, stop=False)

            def step_w(i, lhs, start, stop):
                w = weights_of(i)
                for c in range(KC):
                    for h in range(2):
                        ins = mm(acc[h * N:(h + 1) * N, :], lhs(c), w[:, c, h * HD:(h + 1) * HD],
                                 start=start and c == 0, stop=stop and c == KC - 1)
                ins.then_inc(used, 1)

            def transposed(src, rhs, done):
                for c in range(KC):
                    h, k = c % 2, c // 2
                    ins = mm(xt_ps[h][:, k * N:(k + 1) * N], src[h * N:(h + 1) * N, k * P:(k + 1) * P],
                             rhs[h * N:(h + 1) * N, :], start=True, stop=True)
                ins.then_inc(done, 1)

            pe.wait_ge(hot3_ready, 3)
            for t in range(ET):
                ins = mm(ps_t[:, 0, 0:R3 * N], hot_src[0:EP, t, :], hot3[0:EP, t, :], start=t == 0, stop=t == ET - 1)
            ins.then_inc(counts3, 1)
            pe.wait_ge(a3_copied, 1)
            mm(ps_t[:, 1, 0:R3 * N], one[0:N, :], a3[0:N, :], start=True, stop=True).then_inc(cnt3_ps, 1)
            pe.wait_ge(csd_ready, 1)
            mm(ps_x[:, 0:N], c_sd[0:N, :, :].rearrange("p a n -> p (a n)"), eye[0:N, :], start=True, stop=True)
            mm(ps_x[:, N:2 * N], one[0:N, :], c_sd[0:N, 0, :], start=True, stop=True).then_inc(cds_ps, 1)

            pe.wait_ge(bias_in, 16)
            wq = weights_of(1)
            pe.wait_ge(loaded[RING[0][0]], 16)
            qt = slot(0)[:, 0:KC * B * L].rearrange("p (c r) -> p c r", c=KC)
            for k in range(B // 2):
                if k >= 2:
                    pe.wait_ge(qg_copied_v, k - 1)
                for h in range(2):
                    dst = ps_g[:, 2 * (k % 2) + h, 0:HD]
                    mm(dst, cst[0:len(BIAS), C_BIAS + BG * N:C_BIAS + (BG + 2) * N],
                       bias_rows[:, h * HD:(h + 1) * HD], start=True, stop=False)
                    for c in range(KC):
                        ins = mm(dst, qt[:, c, k * P:(k + 1) * P], wq[:, c, h * HD:(h + 1) * HD],
                                 start=False, stop=c == KC - 1)
                if k == B // 2 - 1:
                    ins.then_inc(used, 2)
                else:
                    ins.then_inc(qg_ps, 1)
            pe.wait_ge(hot8_ready, 1)
            for t in range(ET):
                ins = mm(ps_t[:, 0, :], hot_src[0:EP, t, :], hot8[0:EP, t, :], start=t == 0, stop=t == ET - 1)
            ins.then_inc(counts8, 1)
            pe.wait_ge(a8_copied, 1)
            mm(ps_acc[:, :], one[0:N, :], a8[0:N, :], start=True, stop=True).then_inc(cnt8_ps, 1)

            def conv(name, load, src, adj, rels, bias_i, root):
                if name == "rgcn1":
                    pe.wait_ge(x_in, 32)
                else:
                    pe.wait_ge(state[name], 1)
                transposed(src, eye if root else adj, xt_done[name])
                if rels:
                    for c in range(KC):
                        h, k = c % 2, c // 2
                        if k >= 2:
                            pe.wait_ge(mt_a[name] if h else mt_v[name], k - 1)
                        mm(ps_g[:, 2 * (k % 2) + h, 0:rels * N], src[h * N:(h + 1) * N, k * P:(k + 1) * P],
                           adj[h * N:(h + 1) * N, :], start=True, stop=True).then_inc(mt_done[name][h], 1)
                pe.wait_ge(xt_copied[name], 2)
                bias(bias_i)
                step_w(load, lambda c: xt[:, c * N:(c + 1) * N], False, not rels)
                if rels:
                    pe.wait_ge(mt_v[name], KC // 2)
                    pe.wait_ge(mt_a[name], KC // 2)
                    for r in range(rels):
                        step_w(load + 1 + r, lambda c: mt[:, (c * rels + r) * N:(c * rels + r + 1) * N], False, r == rels - 1)

            def gate(g, load):
                pe.wait_ge(h_ready[g], 1)
                transposed(xs["a"], eye, ht_done[g])
                pe.wait_ge(ht_copied[g], 2)
                step_w(load, lambda c: xt[:, c * N:(c + 1) * N], True, True)
                pe.wait_ge(hg_split[g], 4)
                pe.wait_ge(query_in, 32)
                pe.wait_ge(sel_ready, 5)
                pe.wait_ge(qg_copied_v, B // 2)
                pe.wait_ge(qg_copied_a, B // 2)

                def add(t):
                    b = t // (TILES // B)
                    if t >= 2:
                        pe.wait_ge(tile_sig[g], t - 1)
                    for h in range(2):
                        dst = ps_g[:, 2 * (t % 2) + h, 0:HD]
                        mm(dst, eye_b[:, :], qg_hm[:, b, h * HD:(h + 1) * HD], start=True, stop=False)
                        mm(dst, sel_node[:, t * P:(t + 1) * P], hg_hm[:, h, :], start=False, stop=False)
                        ins = mm(dst, sel_low[h][:, t * P:(t + 1) * P], lows[:, b, h, :], start=False, stop=True)
                    ins.then_inc(tile_sum[g], 1)

                def reduce(t):
                    pe.wait_ge(tile_prod[g], t + 1)
                    w0 = C_SUM + N - 2 - 2 * t
                    for h in range(2):
                        ins = mm(ps_qi[h * N:(h + 1) * N, :], cst[:, w0:w0 + N], prod[:, t % 2, h * HD:(h + 1) * HD],
                                 start=t == 0, stop=t == TILES - 1)
                    ins.then_inc(tile_red[g], 1)

                for t in range(TILES + 2):
                    if t < TILES:
                        add(t)
                    if t >= 2:
                        reduce(t - 2)
                    if t == TILES:
                        bias("L0_bq")
                        step_w(load + 1, lambda c: xt[:, c * N:(c + 1) * N], False, False)
                pe.wait_ge(qi_copied[g], 1)
                transposed(qi, eye, qit_done[g])
                pe.wait_ge(qit_copied[g], 2)
                step_w(load + 2, lambda c: qit[:, c * N:(c + 1) * N], False, True)

            def norm(n):
                pe.wait_ge(mv_ready[n], 1)
                mm(ps_s[:, 0:2], cst[:, C_AVG:C_AVG + P], mv[:, :], start=True, stop=True)
                mm(ps_s[:, 2:3], cst[:, C_DIF:C_DIF + P], mv[:, 0:1], start=True, stop=True).then_inc(mv_ps[n], 1)

            def attend(name, bias_i):
                pe.wait_ge(parts_ready[name], 3)
                mm(ps_s[:, 0:N], one, diag[:, :], start=True, stop=True)
                mm(ps_s[:, N:N + 1], cst[:, C_PAIR:C_PAIR + P], a_part[:, 1:2], start=True, stop=True).then_inc(logits_ps[name], 1)
                bias(bias_i)
                pe.wait_ge(alpha_ready[name], 1)
                mm(ps_x[:, 0:N], e_t[0:N, 3:5, :].rearrange("p a n -> p (a n)"), eye[0:N, :],
                   start=True, stop=True).then_inc(alphat_ps[name], 1)
                pe.wait_ge(alphat_ready[name], 2)
                for h in range(2):
                    ins = mm(acc[h * N:(h + 1) * N, :], al_t[:, h, :], qi[:, :], start=False, stop=True)
                ins.then_inc(mix_done[name], 1)

            load = 2
            pe.wait_ge(a3_ready, 1)
            conv("rgcn1", load, xs["in"], a3[:, :], R3, "L0_b1", True)
            gate("g1", load + 4)
            load += 7
            conv("rgcn2", load, xs["b"], a3[:, :], R3, "L0_b2", True)
            gate("g2", load + 4)
            load += 7
            norm("n0")
            conv("gcn1", load, xs["in"], ahat[:, :], 0, "L1_b1", False)
            conv("gcn2", load + 1, xs["a"], ahat[:, :], 0, "L1_b2", False)
            norm("n1")
            for k, name in enumerate(gats):
                src = xs["in"] if k == 0 else xs["a"]
                pe.wait_ge(state[name], 1)
                transposed(src, eye, xt_done[name])
                pe.wait_ge(xt_copied[name], 2)
                step_w(load + 2 + k, lambda c: xt[:, c * N:(c + 1) * N], True, True)
                attend(name, f"L2_b{k + 1}")
            norm("n2")
            load += 4
            conv("r8a", load, xs["in"], a8[:, :], R8, "L3_b1", True)
            conv("r8b", load + 1 + R8, xs["a"], a8[:, :], R8, "L3_b2", True)
            norm("n3")

        @block.scalar
        def _(act):
            copy = nc.scalar.copy
            half_t = slice(3 * N, 6 * N)

            act.wait_ge(const_in, 16)
            nc.scalar.activation(table[:, :], cst[:, 0:1], ACT.Sigmoid)
            for k in range(B // 2):
                if k < B // 2 - 1:
                    act.wait_ge(qg_ps, k + 1)
                else:
                    act.wait_ge(used, 2)
                src = ps_g[:, 2 * (k % 2):2 * (k % 2) + 2, 0:HD]
                for hh in range(2):
                    r = slice(hh * N, (hh + 1) * N)
                    ins = copy(qg_hm[r, 2 * k + hh, :].rearrange("p (h f) -> p h f", h=2), src[r, :, :])
                ins.then_inc(qg_copied_a, 1)

            def t_copy(name, rels):
                act.wait_ge(xt_done[name], 1)
                copy(xt[:, half_t], xt_ps[1]).then_inc(xt_copied[name], 1)
                for k in range(3 if rels else 0):
                    c = 3 + k
                    act.wait_ge(mt_done[name][1], k + 1)
                    copy(mt[:, c * rels * N:(c + 1) * rels * N], ps_g[:, 2 * (k % 2) + 1, 0:rels * N]).then_inc(mt_a[name], 1)

            def gate(g):
                act.wait_ge(ht_done[g], 1)
                copy(xt[:, half_t], xt_ps[1]).then_inc(ht_copied[g], 1)
                for t in range(TILES):
                    act.wait_ge(tile_sum[g], t + 1)
                    if t >= 2:
                        act.wait_ge(tile_prod[g], t - 1)
                    nc.scalar.activation(att_s[:, t % 2, :].rearrange("p (h f) -> p h f", h=2),
                                         ps_g[:, 2 * (t % 2):2 * (t % 2) + 2, 0:HD], ACT.Sigmoid).then_inc(tile_sig[g], 1)
                act.wait_ge(tile_red[g], TILES)
                act.wait_ge(qi_copied[g], 1)
                nc.scalar.activation(th[:, :], qi[:, :], ACT.Tanh).then_inc(tanh_done[g], 1)
                act.wait_ge(qit_done[g], 1)
                copy(qit[:, half_t], xt_ps[1]).then_inc(qit_copied[g], 1)
                act.wait_ge(used, last_of(f"al_{g}"))
                nc.scalar.activation(alpha[:, :], acc, ACT.Sigmoid).then_inc(al_done[g], 1)

            t_copy("rgcn1", R3)
            gate("g1")
            t_copy("rgcn2", R3)
            gate("g2")
            t_copy("gcn1", 0)
            t_copy("gcn2", 0)
            for name in gats:
                t_copy(name, 0)
                act.wait_ge(exp_in[name], 1)
                nc.scalar.activation(e_t[:, 1, :], e_t[:, 0, :], ACT.Exp, bias=st[:, 7:8]).then_inc(exp_done[name], 1)
            t_copy("r8a", R8)
            t_copy("r8b", R8)

        @block.vector
        def _(dve):
            v = nc.vector
            made = [0]

            def link(ins):
                made[0] += 1
                ins.then_inc(vec, 1)
                dve.wait_ge(vec, made[0])

            def tell(ins, s, value=1):
                ins.then_inc(s, 1)
                dve.wait_ge(s, value)

            half_t = slice(0, 3 * N)
            f_src, f_dst, f_t3, f_t8 = (edges_f[:, k, :] for k in range(4))

            dve.wait_ge(edges_in, 16)
            link(v.tensor_copy(edges_f[:, :, :], edges_i[:, :, :]))
            link(v.scalar_tensor_tensor(out=keys[:, 0, :], in0=f_t3, scalar=float(N), in1=f_dst, op0=ALU.mult, op1=ALU.add))
            link(v.scalar_tensor_tensor(out=keys[:, 1, :], in0=f_t8, scalar=float(N), in1=f_dst, op0=ALU.mult, op1=ALU.add))
            dve.wait_ge(const_in, 16)
            link(v.tensor_copy(eye_b[:, 0:N], eye))
            v.tensor_copy(eye_b[:, N:P], eye).then_inc(hot3_ready, 1)
            v.tensor_tensor(hot_src[0:EP, :, :].rearrange("p t (a n) -> p t a n", a=2),
                            f_src.unsqueeze(2).unsqueeze(3).to_broadcast([EP, ET, 2, N]),
                            iota[:, 0:N].unsqueeze(1).unsqueeze(1).to_broadcast([EP, ET, 2, N]),
                            ALU.is_equal).then_inc(hot3_ready, 1)
            v.tensor_tensor(hot3[0:EP, :, :], keys[:, 0, :].unsqueeze(2).to_broadcast([EP, ET, R3 * N]),
                            iota[:, 0:R3 * N].unsqueeze(1).to_broadcast([EP, ET, R3 * N]),
                            ALU.is_equal).then_inc(hot3_ready, 1)
            dve.wait_ge(counts3, 1)
            tell(v.tensor_copy(a3[:, :], ps_t[:, 0, 0:R3 * N]), a3_copied)
            link(v.tensor_tensor(mask[:, :], a3[:, 0:N], a3[:, N:2 * N], ALU.add))
            link(v.tensor_tensor(far[:, :], a3[:, 2 * N:3 * N], eye, ALU.add))
            tell(v.tensor_tensor(c_sd[:, :, :], mask[:, :].unsqueeze(1).to_broadcast([P, 2, N]),
                                 far[:, :].unsqueeze(1).to_broadcast([P, 2, N]), ALU.add), csd_ready)
            dve.wait_ge(cnt3_ps, 1)
            link(v.tensor_scalar(cnt3[:, :], ps_t[:, 1, 0:R3 * N], 1.0, None, ALU.max))
            link(v.reciprocal(cnt3[:, :], cnt3[:, :]))
            tell(v.tensor_tensor(a3[:, :], a3[:, :], cnt3[:, :], ALU.mult), a3_ready)
            dve.wait_ge(cds_ps, 1)
            link(v.tensor_copy(c_ds[:, :], ps_x[:, 0:N]))
            link(v.tensor_reduce(deg[:, :], c_ds[:, :], AX.X, ALU.add))
            v.tensor_copy(dinv_row[:, :], ps_x[:, N:2 * N]).then_inc(deg_ready, 1)
            dve.wait_ge(dinv_ready, 2)
            link(v.scalar_tensor_tensor(out=ahat[:, :], in0=c_sd[:, 0, :], scalar=dinv_col[:, :], in1=dinv_row[:, :],
                                        op0=ALU.mult, op1=ALU.mult))
            link(v.tensor_scalar(mask[:, :], c_ds[:, :], 0.0, None, ALU.is_gt))
            link(v.tensor_scalar(far[:, :], mask[:, :], 1.0, FAR, ALU.subtract, ALU.mult))
            v.tensor_tensor(hot8[0:EP, :, :], keys[:, 1, :].unsqueeze(2).to_broadcast([EP, ET, R8 * N]),
                            iota.unsqueeze(1).to_broadcast([EP, ET, R8 * N]), ALU.is_equal).then_inc(hot8_ready, 1)
            for k in range(B // 2):
                dve.wait_ge(qg_copied_a, k + 1)
                src = ps_g[:, 2 * (k % 2):2 * (k % 2) + 2, 0:HD]
                for hh in range(2):
                    r, other = slice(hh * N, (hh + 1) * N), slice((1 - hh) * N, (2 - hh) * N)
                    b = 2 * k + hh
                    hi = qg_hm[r, b, :].rearrange("p (h f) -> p h f", h=2)
                    for h in range(2):
                        rest, m = x_low[r, :], mid[r, :]
                        link(v.tensor_tensor(rest, src[r, h, :], hi[:, h, :], ALU.subtract))
                        link(v.tensor_copy(m, rest))
                        link(v.tensor_copy(qg_hm[other, b, h * HD:(h + 1) * HD], m))
                        to = slice(N, P) if h == 0 else slice(0, N)
                        link(v.tensor_tensor(low[r, :], rest, m, ALU.subtract))
                        ins = v.tensor_copy(lows[to, b, h, :], low[r, :])
                        if hh == 1 and h == 1:
                            dve.wait_ge(vec, made[0])
                            ins.then_inc(qg_copied_v, 1)
                        else:
                            link(ins)
            dve.wait_ge(counts8, 1)
            tell(v.tensor_copy(a8[:, :], ps_t[:, 0, :]), a8_copied)
            dve.wait_ge(cnt8_ps, 1)
            link(v.tensor_scalar(cnt8[:, :], ps_acc[:, :], 1.0, None, ALU.max))
            link(v.reciprocal(cnt8[:, :], cnt8[:, :]))
            tell(v.tensor_tensor(a8[:, :], a8[:, :], cnt8[:, :], ALU.mult), a8_ready)

            def t_copy(name, rels):
                dve.wait_ge(xt_done[name], 1)
                v.tensor_copy(xt[:, half_t], xt_ps[0]).then_inc(xt_copied[name], 1)
                for c in range(3 if rels else 0):
                    dve.wait_ge(mt_done[name][0], c + 1)
                    v.tensor_copy(mt[:, c * rels * N:(c + 1) * rels * N], ps_g[:, 2 * (c % 2), 0:rels * N]).then_inc(mt_v[name], 1)

            def relu(name, done):
                if name in gats:
                    dve.wait_ge(mix_done[name], 1)
                else:
                    dve.wait_ge(used, last_of(name))
                v.tensor_scalar(xs["a"][:, :], acc, 0.0, None, ALU.max).then_inc(done, 1)

            def gate(g):
                h = xs["a"]
                dve.wait_ge(ht_done[g], 1)
                v.tensor_copy(xt[:, half_t], xt_ps[0]).then_inc(ht_copied[g], 1)
                dve.wait_ge(used, last_of(f"hg_{g}"))
                v.tensor_copy(hg_hm[0:N, 0, :], acc[0:N, :])
                link(v.tensor_copy(hg_hm[N:P, 1, :], acc[N:P, :]))
                v.tensor_tensor(x_low[0:N, :], acc[0:N, :], hg_hm[0:N, 0, :], ALU.subtract)
                link(v.tensor_tensor(x_low[N:P, :], acc[N:P, :], hg_hm[N:P, 1, :], ALU.subtract))
                link(v.tensor_copy(mid[:, :], x_low[:, :]))
                v.tensor_copy(hg_hm[N:P, 0, :], mid[0:N, :]).then_inc(hg_split[g], 1)
                v.tensor_copy(hg_hm[0:N, 1, :], mid[N:P, :]).then_inc(hg_split[g], 1)
                link(v.tensor_tensor(low[:, :], x_low[:, :], mid[:, :], ALU.subtract))
                for r, k in ((slice(0, N), 0), (slice(N, P), 1)):
                    v.tensor_copy(lows[r, :, k, :], low[r, :].unsqueeze(1).to_broadcast([N, B, HD])).then_inc(hg_split[g], 1)
                for t in range(TILES):
                    b = t // (TILES // B)
                    dve.wait_ge(tile_sig[g], t + 1)
                    if t >= 2:
                        dve.wait_ge(tile_red[g], t - 1)
                    v.tensor_tensor(prod[:, t % 2, :], att_s[:, t % 2, :], q_rows[:, b, :], ALU.mult).then_inc(tile_prod[g], 1)
                dve.wait_ge(tile_red[g], TILES)
                v.tensor_copy(qi[:, :], ps_qi).then_inc(qi_copied[g], 1)
                dve.wait_ge(qit_done[g], 1)
                v.tensor_copy(qit[:, half_t], xt_ps[0]).then_inc(qit_copied[g], 1)
                dve.wait_ge(tanh_done[g], 1)
                link(v.tensor_tensor(th[:, :], th[:, :], h[:, :], ALU.subtract))
                dve.wait_ge(al_done[g], 1)
                link(v.tensor_tensor(alpha[:, :], alpha[:, :], th[:, :], ALU.mult))

            def norm(n, done, dst):
                y = xs["y"]
                link(v.bn_stats(stat[:, :], y[:, :]))
                v.bn_aggr(mv[:, :], stat[:, :]).then_inc(mv_ready[n], 1)
                dve.wait_ge(mv_ps[n], 1)
                link(v.tensor_copy(st[:, 0:3], ps_s[:, 0:3]))
                link(v.tensor_scalar(st[:, 5:6], ps_s[:, 1:2], EPS, None, ALU.add))
                v.scalar_tensor_tensor(out=st[:, 3:4], in0=st[:, 2:3], scalar=st[:, 2:3], in1=st[:, 5:6],
                                       op0=ALU.mult, op1=ALU.add).then_inc(var_ready[n], 1)
                dve.wait_ge(rstd_ready[n], 1)
                v.tensor_scalar(dst[:, :], y[:, :], st[:, 0:1], st[:, 4:5], ALU.subtract, ALU.mult).then_inc(done, 1)

            t_copy("rgcn1", R3)
            relu("rgcn1", h_ready["g1"])
            gate("g1")
            v.tensor_tensor(xs["b"][:, :], alpha[:, :], xs["a"][:, :], ALU.add).then_inc(state["rgcn2"], 1)
            t_copy("rgcn2", R3)
            relu("rgcn2", h_ready["g2"])
            gate("g2")
            link(v.tensor_tensor(alpha[:, :], alpha[:, :], xs["a"][:, :], ALU.add))
            link(v.tensor_tensor(xs["y"][:, :], alpha[:, :], xs["in"][:, :], ALU.add))
            norm("n0", state["gcn1"], xs["in"])
            t_copy("gcn1", 0)
            relu("gcn1", state["gcn2"])
            t_copy("gcn2", 0)
            dve.wait_ge(used, last_of("gcn2"))
            dve.wait_ge(state["gcn1"], 1)
            link(v.tensor_tensor(xs["y"][:, :], acc, xs["in"][:, :], ALU.add))
            norm("n1", state["gat1"], xs["in"])
            dve.wait_ge(att_in, 16 * 8)
            link(v.memset(al_t[:, :, :], 0.0))
            for k, name in enumerate(gats):
                t_copy(name, 0)
                dve.wait_ge(used, last_of(name))
                link(v.tensor_copy(qi[:, :], acc))
                for a in range(2):
                    tell(v.tensor_tensor_reduce(x_low[:, :], qi[:, :], att_rows[:, 2 * k + a, :], 1.0, 0.0,
                                                ALU.mult, ALU.add, a_part[:, a:a + 1]), parts_ready[name], a + 1)
                v.tensor_scalar(diag[:, :], eye, a_part[:, 0:1], None, ALU.mult).then_inc(parts_ready[name], 1)
                dve.wait_ge(logits_ps[name], 1)
                link(v.tensor_copy(st[:, 5:6], ps_s[:, N:N + 1]))
                link(v.tensor_scalar(e_t[:, 0, :], ps_s[:, 0:N], st[:, 5:6], None, ALU.add))
                link(v.scalar_tensor_tensor(out=e_t[:, 2, :], in0=e_t[:, 0, :], scalar=SLOPE, in1=e_t[:, 0, :],
                                            op0=ALU.mult, op1=ALU.max))
                link(v.tensor_tensor(e_t[:, 2, :], e_t[:, 2, :], mask[:, :], ALU.mult))
                link(v.tensor_tensor(e_t[:, 0, :], e_t[:, 2, :], far[:, :], ALU.add))
                link(v.tensor_reduce(st[:, 6:7], e_t[:, 0, :], AX.X, ALU.max))
                v.tensor_scalar(st[:, 7:8], st[:, 6:7], -1.0, None, ALU.mult).then_inc(exp_in[name], 1)
                dve.wait_ge(exp_done[name], 1)
                link(v.tensor_tensor_reduce(e_t[:, 2, :], e_t[:, 1, :], c_ds[:, :], 1.0, 0.0, ALU.mult, ALU.add, st[:, 5:6]))
                link(v.reciprocal(st[:, 6:7], st[:, 5:6]))
                v.tensor_scalar(e_t[:, 3:5, :], e_t[:, 2, :].unsqueeze(1).to_broadcast([P, 2, N]), st[:, 6:7], None, ALU.mult).then_inc(alpha_ready[name], 1)
                dve.wait_ge(alphat_ps[name], 1)
                for h in range(2):
                    r = slice(h * N, (h + 1) * N)
                    v.tensor_copy(al_t[r, h, :], ps_x[r, 0:N]).then_inc(alphat_ready[name], 1)
                if k == 0:
                    relu(name, state["gat2"])
            dve.wait_ge(mix_done["gat2"], 1)
            dve.wait_ge(state["gat1"], 1)
            link(v.tensor_tensor(xs["y"][:, :], acc, xs["in"][:, :], ALU.add))
            norm("n2", state["r8a"], xs["in"])
            t_copy("r8a", R8)
            relu("r8a", state["r8b"])
            t_copy("r8b", R8)
            dve.wait_ge(used, last_of("r8b"))
            dve.wait_ge(state["r8a"], 1)
            link(v.tensor_tensor(xs["y"][:, :], acc, xs["in"][:, :], ALU.add))
            norm("n3", result, xs["y"])


def kernel(**inputs):
    import concourse.bacc as bacc
    from concourse.bass_utils import run_bass_kernel_spmd

    get = {k: np.asarray(v) for k, v in inputs.items()}

    def chunked(w):
        return w.reshape(KC, P, -1).transpose(1, 0, 2).reshape(P, -1)

    mats = {"root1": get["L0_gnn_W_root1"], "root2": get["L0_gnn_W_root2"],
            "Wg_h": get["L0_gnn_Wg"][:, :D].T, "Wg_q": get["L0_gnn_Wg"][:, D:].T,
            "Wq_h": get["L0_gnn_Wq"][:, :D].T, "Wq_q": get["L0_gnn_Wq"][:, D:].T,
            "gcn1": get["L1_gnn_W1"], "gcn2": get["L1_gnn_W2"], "gat1": get["L2_gnn_W1"], "gat2": get["L2_gnn_W2"],
            "r8a_root": get["L3_gnn_root1"], "r8b_root": get["L3_gnn_root2"]}
    for r in range(R3):
        mats[f"rel1_{r}"], mats[f"rel2_{r}"] = get["L0_gnn_W_rel1"][r], get["L0_gnn_W_rel2"][r]
    for r in range(R8):
        mats[f"r8a_{r}"], mats[f"r8b_{r}"] = get["L3_gnn_W1"][r], get["L3_gnn_W2"][r]
    query = get["L0_gnn_query_embs"]
    biases = [get[k.replace("_", "_gnn_")] for k in BIAS]
    att = [get[k] for k in ("L2_gnn_att_src1", "L2_gnn_att_dst1", "L2_gnn_att_src2", "L2_gnn_att_dst2")]
    edges = np.stack([get[k].reshape(EP, ET) for k in ("src", "dst", "edge_type_3", "edge_type_8")], 1)
    arrays = {
        "x": get["x"],
        "edges": edges,
        "consts": constants(),
        "biases": np.stack(biases),
        "query_t": chunked(query.reshape(B * L, D).T),
        "query": np.ascontiguousarray(query.transpose(1, 0, 2)),
        "att": np.stack(att),
        "weights": np.stack([chunked(mats[n]) for n in NAMES]),
    }
    arrays = {k: np.ascontiguousarray(v) for k, v in arrays.items()}
    nc = bacc.Bacc("TRN2", target_bir_lowering=False, num_devices=1)
    args = [nc.dram_tensor(f"in_{k}", a.shape, mybir.dt.from_np(a.dtype), kind="ExternalInput").ap() for k, a in arrays.items()]
    out = nc.dram_tensor("out", (N, D), F32, kind="ExternalOutput").ap()
    build(nc, *args, out)
    r = run_bass_kernel_spmd(nc, [{f"in_{k}": a for k, a in arrays.items()}], core_ids=[0])
    return r.results[0]["out"]
```

```python
from contextlib import ExitStack

import concourse.bass as bass
import numpy as np
from concourse import mybir

F32 = mybir.dt.float32
BF16 = mybir.dt.bfloat16
I32 = mybir.dt.int32
ALU = mybir.AluOpType
ACT = mybir.ActivationFunctionType
AX = mybir.AxisListType

P = 128
N = 64
D = 768
HD = D // 2
KC = D // P
E = 2112
EP = 96
ET = E // EP
B, L = 8, 64
NB = N // B
TILES = N // 2
EPS = 1e-5
SLOPE = 0.2
R3, R8 = 3, 8
MAT = KC * D
FAR = 1e30

NAMES = (["rel1_0", "rel1_1", "rel1_2", "root1", "rel2_0", "rel2_1", "rel2_2", "root2",
          "Wg_h", "Wg_q", "Wq_h", "Wq_q", "gcn1", "gcn2", "gat1", "gat2"]
         + [f"r8a_{r}" for r in range(R8)] + ["r8a_root"] + [f"r8b_{r}" for r in range(R8)] + ["r8b_root"])
LOADS = (["Q", "Wg_q", "root1", "rel1_0", "rel1_1", "rel1_2", "Wg_h", "Wq_h", "Wq_q",
          "root2", "rel2_0", "rel2_1", "rel2_2", "Wg_h", "Wq_h", "Wq_q", "gcn1", "gcn2", "gat1", "gat2",
          "r8a_root"] + [f"r8a_{r}" for r in range(R8)] + ["r8b_root"] + [f"r8b_{r}" for r in range(R8)])
FIRST_SLOTS = 5
ALL_SLOTS = 8
WIDE_FROM = LOADS.index("gat2")

BIAS = ["L0_b1", "L0_b2", "L0_bq", "L1_b1", "L1_b2", "L2_b1", "L2_b2", "L3_b1", "L3_b2", "L0_bg"]

C_EYE = 0
C_SUM = C_EYE + N
C_AVG = C_SUM + 2 * N - 2
C_DIF = C_AVG + P
C_PAIR = C_DIF + P
C_ONE = C_PAIR + P
C_END = C_ONE + P
Q_TILES = TILES // B
S_EYE = 0
S_SEL = S_EYE + P
S_GATHER = S_SEL + Q_TILES * P
G_WIDTH = P + 2 * NB
S_END = S_GATHER + 4 * G_WIDTH
BF16_ONE = 0x3F80


def constants():
    c = np.zeros((P, C_END), np.float32)
    p = np.arange(P)
    same = (p[:, None] % N == p[None, :] % N).astype(np.float32)
    c[:, C_EYE:C_EYE + N] = same[:, :N]
    c[:N, C_SUM + N - 2] = 1
    c[N:, C_SUM + N - 1] = 1
    c[:, C_AVG:C_AVG + P] = same / 2
    c[:, C_DIF:C_DIF + P] = np.eye(P, dtype=np.float32) - same / 2
    c[:, C_PAIR:C_PAIR + P] = same
    c[:, C_ONE:C_ONE + P] = 1
    return c


def bf16_constants():
    s = np.zeros((P, S_END), np.uint16)
    one = np.uint16(BF16_ONE)
    p = np.arange(P)
    s[:, S_EYE:S_EYE + P][p[:, None] % N == p[None, :] % N] = one
    for k in range(Q_TILES):
        for i in range(2):
            col = S_SEL + k * P + i * N
            s[np.arange(N), col + np.arange(N)] = one
            for part in range(3):
                s[N + NB * part + 2 * k + i, col:col + N] = one
    for g in range(2):
        for h in range(2):
            col = S_GATHER + (2 * g + h) * G_WIDTH + 2 * NB
            for j in range(4):
                for n in range(NB):
                    s[h * N + (4 * g + j) * NB + n, col + 32 * j + n] = one
    return s


def bias_picks():
    c = np.zeros((len(BIAS), len(BIAS) * N), np.float32)
    for i in range(len(BIAS)):
        c[i, i * N:(i + 1) * N] = 1
    return c


def ring():
    slots, held, uses, out = [], {}, {}, []
    for i in range(len(LOADS)):
        if i < WIDE_FROM:
            s = i % FIRST_SLOTS
        elif i < WIDE_FROM + ALL_SLOTS - FIRST_SLOTS:
            s = FIRST_SLOTS + i - WIDE_FROM
        else:
            s = slots[i - ALL_SLOTS]
        slots.append(s)
        uses[s] = uses.get(s, 0) + (i >= 2)
        out.append((s, uses[s], held.get(s)))
        held[s] = i
    return out


RING = ring()
KEEP_ALPHA, KEEP_NORM, KEEP_NORM_BIAS, KEEP_PARTS, KEEP_EXP, KEEP_RELU = 6, 8, 3, 6, 12, 4
CONVS = ["rgcn1", "rgcn2", "gcn1", "gcn2", "gat1", "gat2", "r8a", "r8b"]


def build(nc, x, edges, consts, consts16, picks, biases, query_t, query, att, weights, out):
    with ExitStack() as ctx:
        def sb(name, shape, dt=F32):
            return ctx.enter_context(nc.sbuf_tensor(name, shape, dt))

        def sem(name):
            return ctx.enter_context(nc.semaphore(name))

        def sems(what, names):
            return {n: sem(f"{what}_{n}") for n in names}

        ps_t = ctx.enter_context(nc.psum_tensor("ps_t", [P, 2, 512], F32))
        ps_xa = ctx.enter_context(nc.psum_tensor("ps_xa", [P, 2, 512], F32))
        ps_x, ps_acc = ps_xa[:, 0, :], ps_xa[:, 1, :]
        ps_g = ctx.enter_context(nc.psum_tensor("ps_g", [P, 4, 512], F32))
        ps_qi = ps_t[:, :, 0:HD // 2]
        ps_s = ps_t[:, 1, :]
        acc, acc2 = ps_acc[:, 0:HD], ps_t[:, 0, 0:HD]
        acc_alpha = ps_x[:, 0:HD]
        keep = ps_g[:, 3, 0:HD]
        qit_ps = [ps_acc[:, 0:3 * N], ps_t[:, 1, 0:3 * N]]
        xt_ps = [ps_x[:, 0:3 * N], ps_t[:, 1, 0:3 * N]]

        w_ring = sb("w_ring", [P, FIRST_SLOTS, MAT])
        gatebuf = sb("gatebuf", [P, ALL_SLOTS - FIRST_SLOTS, MAT])
        flat = gatebuf[:, :, :].rearrange("p a b -> p (a b)")
        q_rows = flat[:, 0:B * D].rearrange("p (b f) -> p b f", b=B)
        qparts = flat[:, B * D:2 * B * D].bitcast(BF16)
        qg_hm = qparts[:, 0:B * D].rearrange("p (b f) -> p b f", b=B)
        lows = qparts[:, B * D:2 * B * D].rearrange("p (b f) -> p b f", b=B)
        work = sb("work", [P, 6144])
        mt = work[:, 0:KC * 512]
        att_s = work[:, 3072:3072 + 2 * D].rearrange("p (t f) -> p t f", t=2)
        prod = work[:, 3072 + 2 * D:3072 + 4 * D].rearrange("p (t f) -> p t f", t=2)
        hot8 = work[:, 0:ET * R8 * N // 2].bitcast(BF16).rearrange("p (t k) -> p t k", t=ET)
        hot3 = flat[:, 0:ET * R3 * N // 2].bitcast(BF16).rearrange("p (t k) -> p t k", t=ET)
        att_rows = sb("att_rows", [P, 4, HD])
        hot_src = att_rows[:, :, :].rearrange("p a b -> p (a b)")[:, 0:ET * P // 2].bitcast(BF16).rearrange("p (t k) -> p t k", t=ET)
        cst = sb("cst", [P, C_END])
        cst16 = sb("cst16", [P, S_END], mybir.dt.uint16)
        bias_sel = sb("bias_sel", [len(BIAS), len(BIAS) * N])
        bias_rows = sb("bias_rows", [len(BIAS), D])
        after3 = ET * R3 * N // 2
        iota = flat[0:EP, after3:after3 + R8 * N]
        iota_i = flat[0:EP, after3 + R8 * N:after3 + 2 * R8 * N].bitcast(I32)
        edges_i = sb("edges_i", [EP, 4, ET], I32)
        edges_f = sb("edges_f", [EP, 4, ET])
        keys = sb("keys", [EP, 2, ET])
        a3 = sb("a3", [P, R3 * N])
        a8 = sb("a8", [P, R8 * N])
        cnt8 = work[:, ET * R8 * N // 2:ET * R8 * N // 2 + R8 * N]
        c_sd = sb("c_sd", [P, 2, N])
        c_ds = sb("c_ds", [P, N])
        far = sb("far", [P, N])
        mask = sb("mask", [P, N])
        dinv_row = sb("dinv_row", [P, N])
        dinv_col = sb("dinv_col", [P, 1])
        deg = sb("deg", [P, 1])
        ahat = sb("ahat", [P, N])
        xs = {n: sb(f"x_{n}", [P, HD]) for n in ("in", "a", "b", "y")}
        cnt3 = xs["b"][:, 0:R3 * N]
        x_low = sb("x_low", [P, HD])
        parts = flat[:, 2 * B * D:2 * B * D + 2 * HD].bitcast(BF16)
        high = parts[:, 0:2 * HD].rearrange("p (t f) -> p t f", t=2)
        mid, low = parts[:, 2 * HD:3 * HD], parts[:, 3 * HD:4 * HD]
        th = x_low
        qi = sb("qi", [P, HD])
        alpha = xs["b"]
        xt = sb("xt", [P, KC * N])
        qit = sb("qit", [P, KC * N])
        stat = sb("stat", [P, 6])
        mv = sb("mv", [P, 2])
        st = sb("st", [P, 8])
        a_part = sb("a_part", [P, 2])
        diag = sb("diag", [P, N])
        e_t = sb("e_t", [P, 5, N])
        al_t = sb("al_t", [P, 2, N])
        power = sb("power", [P, N])
        table = sb("table", [P, 1])

        eye, one = cst[:, C_EYE:C_EYE + N], cst[:, C_ONE:C_ONE + P]

        def bias_pick(i):
            return bias_sel[:, i * N:(i + 1) * N]

        bits = cst16[:, :].bitcast(BF16)
        eye_b = bits[:, S_EYE:S_EYE + P]

        def sel(k):
            return bits[0:N + 32, S_SEL + k * P:S_SEL + (k + 1) * P]

        def gather(g, h, part):
            at = S_GATHER + (2 * g + h) * G_WIDTH + 2 * NB - NB * part
            return bits[:, at:at + P]

        def last_of(name):
            first = {"rgcn1": 2, "hg_g1": 6, "al_g1": 8, "rgcn2": 9, "hg_g2": 13, "al_g2": 15, "gcn1": 16, "gcn2": 17,
                     "gat1": 18, "gat2": 19, "r8a": 20, "r8b": 20 + R8 + 1}[name]
            return first + 1 + (R3 if name.startswith("rgcn") else R8 if name.startswith("r8") else 0)

        def slot(i):
            s = RING[i][0]
            return w_ring[:, s, :] if s < FIRST_SLOTS else gatebuf[:, s - FIRST_SLOTS, :]

        def gathered_rows(b):
            return (lows[N:N + 32, b, :].rearrange("p (h f) -> p h f", h=2),
                    (ps_t if b < 4 else ps_g[:, 2:4, :])[32 * (b % 4):32 * (b % 4) + 32, :, 0:HD])

        def qi_quarter(h, group, part):
            q = 2 * h + part
            r = h * N + 32 * group
            return qi[r:r + 32, part * HD // 2:(part + 1) * HD // 2], ps_qi[32 * q:32 * q + 32, group, :]

        const_in, edges_in, x_in, bias_in, att_in = (sem(n) for n in ("const_in", "edges_in", "x_in", "bias_in", "att_in"))
        query_in, out_done = sem("query_in"), sem("out_done")
        loaded = [sem(f"loaded_{s}") for s in range(ALL_SLOTS)]
        used = sem("weights_used")
        vec = sem("vec_chain")
        hot3_ready, hot8_ready = sem("hot3_ready"), sem("hot8_ready")
        counts3, counts8 = sem("counts3"), sem("counts8")
        a3_copied, a8_copied = sem("a3_copied"), sem("a8_copied")
        cnt3_ps, cnt8_ps, a3_ready, a8_ready = (sem(n) for n in ("cnt3_ps", "cnt8_ps", "a3_ready", "a8_ready"))
        csd_ready, cds_ps, deg_ready = sem("csd_ready"), sem("cds_ps"), sem("deg_ready")
        q_in, wgq_in = [sem(f"q_in_{k}") for k in range(B // 2)], [sem(f"wgq_in_{h}") for h in range(2)]
        qg_ps, qg_high, qg_read, qg_split = sem("qg_ps"), sem("qg_high"), sem("qg_read"), sem("qg_split")
        qg_mid, qg_placed = sem("qg_mid"), sem("qg_placed")
        const16_in = sem("const16_in")
        state = sems("state", CONVS)
        xt_done = sems("xt_done", CONVS)
        xt_copied = sems("xt_copied", CONVS)
        mt_done = {n: [sem(f"mt_done_{n}_{h}") for h in range(2)] for n in ("rgcn1", "rgcn2", "r8a", "r8b")}
        mt_v = sems("mt_v", ["rgcn1", "rgcn2", "r8a", "r8b"])
        mt_a = sems("mt_a", ["rgcn1", "rgcn2", "r8a", "r8b"])
        gates = ["g1", "g2"]
        h_ready, ht_done, ht_copied, hg_high, hg_split = (sems(n, gates) for n in ("h_ready", "ht_done", "ht_copied", "hg_high", "hg_split"))
        gathered, rows_v, rows_a = (sems(n, gates) for n in ("gathered", "rows_v", "rows_a"))
        qi_v, qi_a = sems("qi_v", gates), sems("qi_a", gates)
        tile_sum, tile_sig, tile_prod, tile_red = (sems(n, gates) for n in ("tile_sum", "tile_sig", "tile_prod", "tile_red"))
        tanh_done, qit_done, qit_copied, al_done = (
            sems(n, gates) for n in ("tanh_done", "qit_done", "qit_copied", "al_done"))
        norms = ["n0", "n1", "n2", "n3"]
        mv_ready, mv_ps, var_ready, rstd_ready = (sems(n, norms) for n in ("mv_ready", "mv_ps", "var_ready", "rstd_ready"))
        dinv_ready, power_set, iota_made = sem("dinv_ready"), sem("power_set"), sem("iota_made")
        gats = ["gat1", "gat2"]
        parts_ready, logits_ps, exp_in, exp_done, alpha_ready, alphat_ps, alphat_ready, mix_done = (
            sems(n, gats) for n in ("parts_ready", "logits_ps", "exp_in", "exp_done", "alpha_ready", "alphat_ps", "alphat_ready", "mix_done"))
        result = sem("result")

        block = ctx.enter_context(nc.Block())

        @block.sync
        def _(sp):
            sp.dma_start(edges_i[:, :, :], edges).then_inc(edges_in, 16)

            def load(i):
                s, _, before = RING[i]
                if before is not None:
                    sp.wait_ge(used, before + 1)
                sp.dma_start(slot(i), weights[NAMES.index(LOADS[i])]).then_inc(loaded[s], 16)

            wq, wq_from = (a.rearrange("p (c n) -> p c n", c=KC) for a in (slot(1), weights[NAMES.index("Wg_q")]))
            for k in range(B // 2):
                if k < 2:
                    cols = slice(k * HD, (k + 1) * HD)
                    sp.dma_start(wq[:, :, cols], wq_from[:, :, cols]).then_inc(wgq_in[k], 16)
                rows = slice(k * D, (k + 1) * D)
                sp.dma_start(slot(0)[:, rows], query_t[:, rows]).then_inc(q_in[k], 16)
                if k == 0:
                    sp.dma_start(cst[:, :], consts).then_inc(const_in, 16)
            sp.dma_start(bias_rows[:, :], biases).then_inc(bias_in, 16)
            sp.dma_start(bias_sel[:, :], picks).then_inc(bias_in, 16)
            sp.dma_start(cst16[:, :], consts16).then_inc(const16_in, 16)
            for h in range(2):
                sp.dma_start(xs["in"][h * N:(h + 1) * N, :], x[:, h * HD:(h + 1) * HD]).then_inc(x_in, 16)
            for i in range(2, FIRST_SLOTS):
                load(i)
            sp.wait_ge(counts3, 1)
            sp.wait_ge(hot8_ready, 2)
            for h in range(2):
                sp.dma_start(q_rows[h * N:(h + 1) * N, :, :], query).then_inc(query_in, 16)
            sp.wait_ge(counts8, 1)
            for k in range(4):
                for h in range(2):
                    sp.dma_start(att_rows[h * N:(h + 1) * N, k, :],
                                 att[k:k + 1, h * HD:(h + 1) * HD].to_broadcast([N, HD])).then_inc(att_in, 16)
            for i in range(FIRST_SLOTS, len(LOADS)):
                if i == WIDE_FROM:
                    sp.wait_ge(tile_red["g2"], TILES)
                load(i)
            sp.wait_ge(result, 1)
            for h in range(2):
                sp.dma_start(out[:, h * HD:(h + 1) * HD], xs["y"][h * N:(h + 1) * N, :]).then_inc(out_done, 16)
            sp.wait_ge(out_done, 32)

        @block.gpsimd
        def _(pool):
            nc.gpsimd.iota(iota_i, [[1, R8 * N]], base=0, channel_multiplier=0).then_inc(iota_made, 1)
            nc.gpsimd.memset(power[:, :], -0.5).then_inc(power_set, 1)
            pool.wait_ge(power_set, 1)
            pool.wait_ge(deg_ready, 1)
            nc.gpsimd.tensor_tensor(dinv_col[:, :], deg[:, :], power[:, 0:1], ALU.pow).then_inc(dinv_ready, 1)
            pool.wait_ge(dinv_ready, 1)
            nc.gpsimd.tensor_tensor(dinv_row[:, :], dinv_row[:, :], power[:, :], ALU.pow).then_inc(dinv_ready, 1)
            pool.wait_ge(dinv_ready, 2)
            for n in norms:
                pool.wait_ge(var_ready[n], 1)
                nc.gpsimd.tensor_tensor(st[:, 4:5], st[:, 3:4], power[:, 0:1], ALU.pow).then_inc(rstd_ready[n], 1)

        @block.tensor
        def _(pe):
            mm = nc.tensor.matmul

            def weights_of(i):
                pe.wait_ge(loaded[RING[i][0]], 16 * RING[i][1])
                return slot(i).rearrange("p (c n) -> p c n", c=KC)

            def bias(name, to):
                i = BIAS.index(name)
                for h in range(2):
                    mm(to[h * N:(h + 1) * N, :], bias_pick(i), bias_rows[:, h * HD:(h + 1) * HD],
                       start=True, stop=False)

            def keep_clock(n):
                for _ in range(n):
                    mm(keep, eye_b, bits[:, 0:HD], start=True, stop=True)

            def step_w(i, lhs, start, stop, to, chunks=range(KC)):
                w = weights_of(i)
                for c in chunks:
                    for h in range(2):
                        ins = mm(to[h * N:(h + 1) * N, :], lhs(c), w[:, c, h * HD:(h + 1) * HD],
                                 start=start and c == 0, stop=stop and c == KC - 1)
                if c == KC - 1:
                    ins.then_inc(used, 1)

            def transposed(src, rhs, done, to=xt_ps):
                for c in range(KC):
                    h, k = c % 2, c // 2
                    ins = mm(to[h][:, k * N:(k + 1) * N], src[h * N:(h + 1) * N, k * P:(k + 1) * P],
                             rhs[h * N:(h + 1) * N, :], start=True, stop=True)
                ins.then_inc(done, 1)

            wq = slot(1).rearrange("p (c n) -> p c n", c=KC)
            qt = slot(0)[:, 0:KC * B * L].rearrange("p (k c r) -> p k c r", k=B // 2, c=KC)
            def query_block(h, k):
                m = h * (B // 2) + k
                if h == 0:
                    pe.wait_ge(q_in[k], 16)
                if k == 0:
                    pe.wait_ge(wgq_in[h], 16)
                if m >= 4:
                    pe.wait_ge(qg_read, m - 3)
                dst = ps_g[:, m % 4, 0:HD]
                for c in range(KC):
                    ins = mm(dst, qt[:, k, c, :], wq[:, c, h * HD:(h + 1) * HD], start=c == 0, stop=c == KC - 1)
                if m == B - 1:
                    ins.then_inc(used, 2)
                else:
                    ins.then_inc(qg_ps, 1)

            query_block(0, 0)
            query_block(0, 1)
            pe.wait_ge(hot3_ready, 2)
            for t in range(ET):
                ins = mm(ps_t[:, 0, 0:R3 * N], hot_src[0:EP, t, :], hot3[0:EP, t, :], start=t == 0, stop=t == ET - 1)
            ins.then_inc(counts3, 1)
            query_block(0, 2)
            query_block(0, 3)
            pe.wait_ge(const_in, 16)
            pe.wait_ge(a3_copied, 1)
            mm(ps_t[:, 1, 0:R3 * N], one[0:N, :], a3[0:N, :], start=True, stop=True).then_inc(cnt3_ps, 1)
            pe.wait_ge(csd_ready, 1)
            mm(ps_x[:, 0:N], c_sd[0:N, :, :].rearrange("p a n -> p (a n)"), eye[0:N, :], start=True, stop=True)
            mm(ps_x[:, N:2 * N], one[0:N, :], c_sd[0:N, 0, :], start=True, stop=True).then_inc(cds_ps, 1)
            for k in range(3):
                query_block(1, k)
            pe.wait_ge(hot8_ready, 2)
            for t in range(ET):
                ins = mm(ps_t[:, 0, :], hot_src[0:EP, t, :], hot8[0:EP, t, :], start=t == 0, stop=t == ET - 1)
            ins.then_inc(counts8, 1)
            query_block(1, 3)
            pe.wait_ge(a8_copied, 1)
            mm(ps_acc[:, :], one[0:N, :], a8[0:N, :], start=True, stop=True).then_inc(cnt8_ps, 1)
            pe.wait_ge(bias_in, 32)
            bias("L0_b1", acc2)

            def conv(name, load, src, adj, rels, to, root):
                if name == "rgcn1":
                    pe.wait_ge(x_in, 32)
                else:
                    pe.wait_ge(state[name], 1)
                transposed(src, eye if root else adj, xt_done[name])
                if rels:
                    for c in range(KC):
                        h, k = c % 2, c // 2
                        if c == 4:
                            pe.wait_ge(xt_copied[name], 2)
                            step_w(load, lambda c: xt[:, c * N:(c + 1) * N], False, False, to)
                        if k >= 2:
                            pe.wait_ge(mt_a[name] if h else mt_v[name], k - 1)
                        mm(ps_g[:, 2 * (k % 2) + h, 0:rels * N], src[h * N:(h + 1) * N, k * P:(k + 1) * P],
                           adj[h * N:(h + 1) * N, :], start=True, stop=True).then_inc(mt_done[name][h], 1)
                if not rels:
                    pe.wait_ge(xt_copied[name], 2)
                    step_w(load, lambda c: xt[:, c * N:(c + 1) * N], False, True, to)
                else:
                    pe.wait_ge(mt_v[name], KC // 2)
                    pe.wait_ge(mt_a[name], KC // 2)
                    for r in range(rels):
                        step_w(load + 1 + r, lambda c: mt[:, (c * rels + r) * N:(c * rels + r + 1) * N], False, r == rels - 1, to)

            def gate(g, load):
                if g == "g1":
                    pe.wait_ge(a8_ready, 1)
                bias("L0_bg", acc)
                pe.wait_ge(h_ready[g], 1)
                transposed(xs["a"], eye, ht_done[g])
                pe.wait_ge(ht_copied[g], 2)
                step_w(load, lambda c: xt[:, c * N:(c + 1) * N], False, True, acc)
                def alpha_of_h(chunks):
                    step_w(load + 1, lambda c: xt[:, c * N:(c + 1) * N], False, False, acc_alpha, chunks)

                bias("L0_bq", acc_alpha)
                alpha_of_h(range(0, 2))
                pe.wait_ge(const16_in, 16)
                for i in range(2):
                    for h in range(2):
                        for part, src in enumerate((high[:, 0, :], mid, low)):
                            if i == 0 and h == 0:
                                pe.wait_ge(*((hg_high[g], 1), (hg_split[g], 1), (hg_split[g], 2))[part])
                            ins = mm((ps_t[:, h, 0:HD] if i == 0 else ps_g[:, 2 + h, 0:HD]), gather(i, h, part), src,
                                     start=part == 0, stop=part == 2)
                    ins.then_inc(gathered[g], 1)
                pe.wait_ge(query_in, 32)
                pe.wait_ge(qg_split, B)
                pe.wait_ge(qg_placed, 4 * B)

                def add(t):
                    b = t // Q_TILES
                    if t % Q_TILES == 0:
                        pe.wait_ge(rows_a[g] if b % 2 else rows_v[g], b // 2 + 1)
                    if t >= 2:
                        pe.wait_ge(tile_sig[g], t - 1)
                    if t == 1:
                        alpha_of_h(range(2, 4))
                        pe.wait_ge(rows_v[g], B // 2)
                        pe.wait_ge(rows_a[g], B // 2)
                    for h in range(2):
                        dst = ps_g[:, 2 * (t % 2) + h, 0:HD]
                        mm(dst, eye_b, qg_hm[:, b, h * HD:(h + 1) * HD], start=True, stop=False)
                        ins = mm(dst, sel(t % Q_TILES), lows[0:N + 32, b, h * HD:(h + 1) * HD], start=False, stop=True)
                    ins.then_inc(tile_sum[g], 1)

                def reduce(t):
                    pe.wait_ge(tile_prod[g], t + 1)
                    if t == 0:
                        pe.wait_ge(rows_v[g], 2)
                        pe.wait_ge(rows_a[g], 2)
                    half = TILES // 2
                    w0 = C_SUM + N - 2 - 2 * (t % half)
                    for q in range(4):
                        ins = mm(ps_qi[32 * q:32 * q + 32, t // half, :], cst[:, w0:w0 + 32],
                                 prod[:, t % 2, q * HD // 2:(q + 1) * HD // 2],
                                 start=t % half == 0, stop=t % half == half - 1)
                    ins.then_inc(tile_red[g], 1)

                for t in range(TILES + 2):
                    if t < TILES:
                        add(t)
                    if t >= 2:
                        reduce(t - 2)
                    if t == TILES:
                        alpha_of_h(range(4, KC))
                pe.wait_ge(qi_v[g], 4)
                pe.wait_ge(qi_a[g], 4)
                transposed(qi, eye, qit_done[g], qit_ps)
                pe.wait_ge(qit_copied[g], 2)
                step_w(load + 2, lambda c: qit[:, c * N:(c + 1) * N], False, True, acc_alpha)

            def norm(n):
                pe.wait_ge(mv_ready[n], 1)
                mm(ps_s[:, 0:2], cst[:, C_AVG:C_AVG + P], mv[:, :], start=True, stop=True)
                mm(ps_s[:, 2:3], cst[:, C_DIF:C_DIF + P], mv[:, 0:1], start=True, stop=True).then_inc(mv_ps[n], 1)

            def attend(name):
                pe.wait_ge(parts_ready[name], 3)
                mm(ps_s[:, 0:N], one, diag[:, :], start=True, stop=True)
                mm(ps_s[:, N:N + 1], cst[:, C_PAIR:C_PAIR + P], a_part[:, 1:2], start=True, stop=True).then_inc(logits_ps[name], 1)
                keep_clock(KEEP_EXP)
                pe.wait_ge(alpha_ready[name], 1)
                mm(ps_x[:, 0:N], e_t[0:N, 3:5, :].rearrange("p a n -> p (a n)"), eye[0:N, :],
                   start=True, stop=True).then_inc(alphat_ps[name], 1)
                pe.wait_ge(alphat_ready[name], 2)
                for h in range(2):
                    ins = mm(acc[h * N:(h + 1) * N, :], al_t[:, h, :], qi[:, :], start=False, stop=True)
                ins.then_inc(mix_done[name], 1)
                if name == "gat1":
                    keep_clock(KEEP_RELU)

            load = 2
            pe.wait_ge(a3_ready, 1)
            pe.wait_ge(qg_read, B)
            conv("rgcn1", load, xs["in"], a3[:, :], R3, acc2, True)
            gate("g1", load + 4)
            load += 7
            bias("L0_b2", acc2)
            keep_clock(KEEP_ALPHA)
            conv("rgcn2", load, xs["b"], a3[:, :], R3, acc2, True)
            gate("g2", load + 4)
            load += 7
            bias("L1_b1", acc2)
            keep_clock(KEEP_ALPHA + KEEP_NORM)
            norm("n0")
            keep_clock(KEEP_NORM)
            conv("gcn1", load, xs["in"], ahat[:, :], 0, acc2, False)
            bias("L1_b2", acc)
            conv("gcn2", load + 1, xs["a"], ahat[:, :], 0, acc, False)
            keep_clock(KEEP_NORM)
            norm("n1")
            keep_clock(KEEP_NORM)
            for k, name in enumerate(gats):
                src = xs["in"] if k == 0 else xs["a"]
                pe.wait_ge(state[name], 1)
                transposed(src, eye, xt_done[name])
                pe.wait_ge(xt_copied[name], 2)
                step_w(load + 2 + k, lambda c: xt[:, c * N:(c + 1) * N], True, True, acc2)
                bias(f"L2_b{k + 1}", acc)
                keep_clock(KEEP_PARTS)
                attend(name)
            bias("L3_b1", acc2)
            keep_clock(KEEP_NORM_BIAS)
            norm("n2")
            keep_clock(KEEP_NORM)
            load += 4
            conv("r8a", load, xs["in"], a8[:, :], R8, acc2, True)
            bias("L3_b2", acc)
            conv("r8b", load + 1 + R8, xs["a"], a8[:, :], R8, acc, True)
            norm("n3")

        @block.scalar
        def _(act):
            copy = nc.scalar.copy
            half_t = slice(3 * N, 6 * N)

            act.wait_ge(power_set, 1)
            nc.scalar.activation(table[:, :], power[:, 0:1], ACT.Sigmoid)
            for m in range(B):
                if m < B - 1:
                    act.wait_ge(qg_ps, m + 1)
                else:
                    act.wait_ge(used, 2)
                if m >= 2:
                    act.wait_ge(qg_split, m - 1)
                copy(high[:, m % 2, :], ps_g[:, m % 4, 0:HD]).then_inc(qg_high, 1)
                h, k = m // (B // 2), m % (B // 2)
                cols = slice(h * HD, (h + 1) * HD)
                act.wait_ge(qg_high, m + 1)
                for hh in range(2):
                    r = slice(hh * N, (hh + 1) * N)
                    copy(qg_hm[r, 2 * k + hh, cols], high[r, m % 2, :]).then_inc(qg_placed, 1)
                act.wait_ge(qg_mid, m + 1)
                for hh in range(2):
                    r, other = slice(hh * N, (hh + 1) * N), slice((1 - hh) * N, (2 - hh) * N)
                    copy(qg_hm[other, 2 * k + hh, cols], mid[r, :]).then_inc(qg_placed, 1)

            def t_copy(name, rels):
                act.wait_ge(xt_done[name], 1)
                copy(xt[:, half_t], xt_ps[1]).then_inc(xt_copied[name], 1)
                for k in range(3 if rels else 0):
                    c = 3 + k
                    act.wait_ge(mt_done[name][1], k + 1)
                    copy(mt[:, c * rels * N:(c + 1) * rels * N], ps_g[:, 2 * (k % 2) + 1, 0:rels * N]).then_inc(mt_a[name], 1)

            def gate(g):
                def gate_sums(group):
                    act.wait_ge(tile_red[g], (group + 1) * TILES // 2)
                    for part in range(2):
                        copy(*qi_quarter(1, group, part)).then_inc(qi_a[g], 1)

                act.wait_ge(ht_done[g], 1)
                copy(xt[:, half_t], xt_ps[1]).then_inc(ht_copied[g], 1)
                act.wait_ge(used, last_of(f"hg_{g}"))
                copy(high[:, 0, :], acc).then_inc(hg_high[g], 1)
                for b in range(1, B, 2):
                    act.wait_ge(gathered[g], b // 4 + 1)
                    copy(*gathered_rows(b)).then_inc(rows_a[g], 1)
                for t in range(TILES):
                    if t == TILES // 2 + 3:
                        gate_sums(0)
                    act.wait_ge(tile_sum[g], t + 1)
                    if t >= 2:
                        act.wait_ge(tile_prod[g], t - 1)
                    nc.scalar.activation(att_s[:, t % 2, :].rearrange("p (h f) -> p h f", h=2),
                                         ps_g[:, 2 * (t % 2):2 * (t % 2) + 2, 0:HD], ACT.Sigmoid).then_inc(tile_sig[g], 1)
                gate_sums(1)
                act.wait_ge(qi_v[g], 4)
                act.wait_ge(qi_a[g], 4)
                nc.scalar.activation(th[:, :], qi[:, :], ACT.Tanh).then_inc(tanh_done[g], 1)
                act.wait_ge(qit_done[g], 1)
                copy(qit[:, half_t], qit_ps[1]).then_inc(qit_copied[g], 1)
                act.wait_ge(used, last_of(f"al_{g}"))
                nc.scalar.activation(alpha[:, :], acc_alpha, ACT.Sigmoid).then_inc(al_done[g], 1)

            t_copy("rgcn1", R3)
            gate("g1")
            t_copy("rgcn2", R3)
            gate("g2")
            t_copy("gcn1", 0)
            t_copy("gcn2", 0)
            for name in gats:
                t_copy(name, 0)
                act.wait_ge(exp_in[name], 1)
                nc.scalar.activation(e_t[:, 1, :], e_t[:, 0, :], ACT.Exp, bias=st[:, 7:8]).then_inc(exp_done[name], 1)
            t_copy("r8a", R8)
            t_copy("r8b", R8)

        @block.vector
        def _(dve):
            v = nc.vector
            made = [0]

            def link(ins):
                made[0] += 1
                ins.then_inc(vec, 1)
                dve.wait_ge(vec, made[0])

            def tell(ins, s, value=1):
                ins.then_inc(s, 1)
                dve.wait_ge(s, value)

            half_t = slice(0, 3 * N)
            f_src, f_dst, f_t3, f_t8 = (edges_f[:, k, :] for k in range(4))

            dve.wait_ge(edges_in, 16)
            link(v.tensor_copy(edges_f[:, :, :], edges_i[:, :, :]))
            dve.wait_ge(iota_made, 1)
            link(v.tensor_copy(iota, iota_i))
            link(v.scalar_tensor_tensor(out=keys[:, 0, :], in0=f_t3, scalar=float(N), in1=f_dst, op0=ALU.mult, op1=ALU.add))
            link(v.scalar_tensor_tensor(out=keys[:, 1, :], in0=f_t8, scalar=float(N), in1=f_dst, op0=ALU.mult, op1=ALU.add))
            v.tensor_tensor(hot_src[0:EP, :, :].rearrange("p t (a n) -> p t a n", a=2),
                            f_src.unsqueeze(2).unsqueeze(3).to_broadcast([EP, ET, 2, N]),
                            iota[:, 0:N].unsqueeze(1).unsqueeze(1).to_broadcast([EP, ET, 2, N]),
                            ALU.is_equal).then_inc(hot3_ready, 1)
            v.tensor_tensor(hot3[0:EP, :, :], keys[:, 0, :].unsqueeze(2).to_broadcast([EP, ET, R3 * N]),
                            iota[:, 0:R3 * N].unsqueeze(1).to_broadcast([EP, ET, R3 * N]),
                            ALU.is_equal).then_inc(hot3_ready, 1)
            def split_block(m):
                h, k = m // (B // 2), m % (B // 2)
                cols = slice(h * HD, (h + 1) * HD)
                dve.wait_ge(qg_high, m + 1)
                hi = high[:, m % 2, :]
                tell(v.tensor_tensor(x_low[:, :], ps_g[:, m % 4, 0:HD], hi, ALU.subtract), qg_read, m + 1)
                if m:
                    dve.wait_ge(qg_placed, 4 * m)
                tell(v.tensor_copy(mid[:, :], x_low[:, :]), qg_mid, m + 1)
                link(v.tensor_tensor(low[:, :], x_low[:, :], mid[:, :], ALU.subtract))
                for hh in range(2):
                    ins = v.tensor_copy(lows[0:N, 2 * k + hh, cols], low[hh * N:(hh + 1) * N, :])
                tell(ins, qg_split, m + 1)

            def one_hot8(half):
                t = slice(half * ET // 2, (half + 1) * ET // 2)
                v.tensor_tensor(hot8[0:EP, t, :], keys[:, 1, t].unsqueeze(2).to_broadcast([EP, ET // 2, R8 * N]),
                                iota.unsqueeze(1).to_broadcast([EP, ET // 2, R8 * N]), ALU.is_equal).then_inc(hot8_ready, 1)

            split_block(0)
            one_hot8(0)
            dve.wait_ge(const_in, 16)
            dve.wait_ge(counts3, 1)
            tell(v.tensor_copy(a3[:, :], ps_t[:, 0, 0:R3 * N]), a3_copied)
            link(v.tensor_tensor(mask[:, :], a3[:, 0:N], a3[:, N:2 * N], ALU.add))
            link(v.tensor_tensor(far[:, :], a3[:, 2 * N:3 * N], eye, ALU.add))
            tell(v.tensor_tensor(c_sd[:, :, :], mask[:, :].unsqueeze(1).to_broadcast([P, 2, N]),
                                 far[:, :].unsqueeze(1).to_broadcast([P, 2, N]), ALU.add), csd_ready)
            split_block(1)
            dve.wait_ge(cnt3_ps, 1)
            link(v.tensor_scalar(cnt3[:, :], ps_t[:, 1, 0:R3 * N], 1.0, None, ALU.max))
            link(v.reciprocal(cnt3[:, :], cnt3[:, :]))
            tell(v.tensor_tensor(a3[:, :], a3[:, :], cnt3[:, :], ALU.mult), a3_ready)
            dve.wait_ge(cds_ps, 1)
            link(v.tensor_copy(c_ds[:, :], ps_x[:, 0:N]))
            link(v.tensor_reduce(deg[:, :], c_ds[:, :], AX.X, ALU.add))
            v.tensor_copy(dinv_row[:, :], ps_x[:, N:2 * N]).then_inc(deg_ready, 1)
            one_hot8(1)
            for m in range(2, B):
                if m == B - 1:
                    dve.wait_ge(counts8, 1)
                    tell(v.tensor_copy(a8[:, :], ps_t[:, 0, :]), a8_copied)
                split_block(m)

            def rest_of_adjacency():
                dve.wait_ge(cnt8_ps, 1)
                link(v.tensor_scalar(cnt8[:, :], ps_acc[:, :], 1.0, None, ALU.max))
                link(v.reciprocal(cnt8[:, :], cnt8[:, :]))
                tell(v.tensor_tensor(a8[:, :], a8[:, :], cnt8[:, :], ALU.mult), a8_ready)
                dve.wait_ge(dinv_ready, 2)
                link(v.scalar_tensor_tensor(out=ahat[:, :], in0=c_sd[:, 0, :], scalar=dinv_col[:, :], in1=dinv_row[:, :],
                                            op0=ALU.mult, op1=ALU.mult))
                link(v.tensor_scalar(mask[:, :], c_ds[:, :], 0.0, None, ALU.is_gt))
                link(v.tensor_scalar(far[:, :], mask[:, :], 1.0, FAR, ALU.subtract, ALU.mult))

            def t_copy(name, rels):
                dve.wait_ge(xt_done[name], 1)
                v.tensor_copy(xt[:, half_t], xt_ps[0]).then_inc(xt_copied[name], 1)
                for c in range(3 if rels else 0):
                    dve.wait_ge(mt_done[name][0], c + 1)
                    v.tensor_copy(mt[:, c * rels * N:(c + 1) * rels * N], ps_g[:, 2 * (c % 2), 0:rels * N]).then_inc(mt_v[name], 1)

            def relu(name, done, src):
                if name in gats:
                    dve.wait_ge(mix_done[name], 1)
                else:
                    dve.wait_ge(used, last_of(name))
                v.tensor_scalar(xs["a"][:, :], src, 0.0, None, ALU.max).then_inc(done, 1)

            def gate(g):
                h = xs["a"]
                dve.wait_ge(ht_done[g], 1)
                v.tensor_copy(xt[:, half_t], xt_ps[0]).then_inc(ht_copied[g], 1)
                dve.wait_ge(used, last_of(f"hg_{g}"))
                dve.wait_ge(hg_high[g], 1)
                link(v.tensor_tensor(x_low[:, :], acc, high[:, 0, :], ALU.subtract))
                tell(v.tensor_copy(mid[:, :], x_low[:, :]), hg_split[g], 1)
                v.tensor_tensor(low[:, :], x_low[:, :], mid[:, :], ALU.subtract).then_inc(hg_split[g], 1)
                for b in range(0, B, 2):
                    dve.wait_ge(gathered[g], b // 4 + 1)
                    v.tensor_copy(*gathered_rows(b)).then_inc(rows_v[g], 1)
                dve.wait_ge(query_in, 32)
                def gate_sums(group):
                    dve.wait_ge(tile_red[g], (group + 1) * TILES // 2)
                    for part in range(2):
                        v.tensor_copy(*qi_quarter(0, group, part)).then_inc(qi_v[g], 1)

                for t in range(TILES):
                    b = t // Q_TILES
                    if t == TILES // 2 + 3:
                        gate_sums(0)
                    dve.wait_ge(tile_sig[g], t + 1)
                    if t >= 2:
                        dve.wait_ge(tile_red[g], t - 1)
                    v.tensor_tensor(prod[:, t % 2, :], att_s[:, t % 2, :], q_rows[:, b, :], ALU.mult).then_inc(tile_prod[g], 1)
                gate_sums(1)
                dve.wait_ge(qit_done[g], 1)
                v.tensor_copy(qit[:, half_t], qit_ps[0]).then_inc(qit_copied[g], 1)
                dve.wait_ge(tanh_done[g], 1)
                link(v.tensor_tensor(th[:, :], th[:, :], h[:, :], ALU.subtract))
                if g == "g2":
                    link(v.tensor_tensor(xs["a"][:, :], xs["a"][:, :], xs["in"][:, :], ALU.add))
                dve.wait_ge(al_done[g], 1)
                link(v.tensor_tensor(alpha[:, :], alpha[:, :], th[:, :], ALU.mult))

            def norm(n, done, dst):
                y = xs["y"]
                link(v.bn_stats(stat[:, :], y[:, :]))
                v.bn_aggr(mv[:, :], stat[:, :]).then_inc(mv_ready[n], 1)
                dve.wait_ge(mv_ps[n], 1)
                link(v.tensor_copy(st[:, 0:3], ps_s[:, 0:3]))
                link(v.tensor_scalar(st[:, 5:6], ps_s[:, 1:2], EPS, None, ALU.add))
                v.scalar_tensor_tensor(out=st[:, 3:4], in0=st[:, 2:3], scalar=st[:, 2:3], in1=st[:, 5:6],
                                       op0=ALU.mult, op1=ALU.add).then_inc(var_ready[n], 1)
                dve.wait_ge(rstd_ready[n], 1)
                v.tensor_scalar(dst[:, :], y[:, :], st[:, 0:1], st[:, 4:5], ALU.subtract, ALU.mult).then_inc(done, 1)

            t_copy("rgcn1", R3)
            rest_of_adjacency()
            relu("rgcn1", h_ready["g1"], acc2)
            gate("g1")
            v.tensor_tensor(xs["b"][:, :], alpha[:, :], xs["a"][:, :], ALU.add).then_inc(state["rgcn2"], 1)
            t_copy("rgcn2", R3)
            relu("rgcn2", h_ready["g2"], acc2)
            gate("g2")
            link(v.tensor_tensor(xs["y"][:, :], alpha[:, :], xs["a"][:, :], ALU.add))
            norm("n0", state["gcn1"], xs["in"])
            t_copy("gcn1", 0)
            relu("gcn1", state["gcn2"], acc2)
            t_copy("gcn2", 0)
            dve.wait_ge(used, last_of("gcn2"))
            dve.wait_ge(state["gcn1"], 1)
            link(v.tensor_tensor(xs["y"][:, :], acc, xs["in"][:, :], ALU.add))
            norm("n1", state["gat1"], xs["in"])
            dve.wait_ge(att_in, 16 * 8)
            link(v.memset(al_t[:, :, :], 0.0))
            for k, name in enumerate(gats):
                t_copy(name, 0)
                dve.wait_ge(used, last_of(name))
                link(v.tensor_copy(qi[:, :], acc2))
                for a in range(2):
                    tell(v.tensor_tensor_reduce(x_low[:, :], qi[:, :], att_rows[:, 2 * k + a, :], 1.0, 0.0,
                                                ALU.mult, ALU.add, a_part[:, a:a + 1]), parts_ready[name], a + 1)
                v.tensor_scalar(diag[:, :], eye, a_part[:, 0:1], None, ALU.mult).then_inc(parts_ready[name], 1)
                dve.wait_ge(logits_ps[name], 1)
                link(v.tensor_copy(st[:, 5:6], ps_s[:, N:N + 1]))
                link(v.tensor_scalar(e_t[:, 0, :], ps_s[:, 0:N], st[:, 5:6], None, ALU.add))
                link(v.scalar_tensor_tensor(out=e_t[:, 2, :], in0=e_t[:, 0, :], scalar=SLOPE, in1=e_t[:, 0, :],
                                            op0=ALU.mult, op1=ALU.max))
                link(v.tensor_tensor(e_t[:, 2, :], e_t[:, 2, :], mask[:, :], ALU.mult))
                link(v.tensor_tensor(e_t[:, 0, :], e_t[:, 2, :], far[:, :], ALU.add))
                link(v.tensor_reduce(st[:, 6:7], e_t[:, 0, :], AX.X, ALU.max))
                v.tensor_scalar(st[:, 7:8], st[:, 6:7], -1.0, None, ALU.mult).then_inc(exp_in[name], 1)
                dve.wait_ge(exp_done[name], 1)
                link(v.tensor_tensor_reduce(e_t[:, 2, :], e_t[:, 1, :], c_ds[:, :], 1.0, 0.0, ALU.mult, ALU.add, st[:, 5:6]))
                link(v.reciprocal(st[:, 6:7], st[:, 5:6]))
                v.tensor_scalar(e_t[:, 3:5, :], e_t[:, 2, :].unsqueeze(1).to_broadcast([P, 2, N]), st[:, 6:7], None, ALU.mult).then_inc(alpha_ready[name], 1)
                dve.wait_ge(alphat_ps[name], 1)
                for h in range(2):
                    r = slice(h * N, (h + 1) * N)
                    v.tensor_copy(al_t[r, h, :], ps_x[r, 0:N]).then_inc(alphat_ready[name], 1)
                if k == 0:
                    relu(name, state["gat2"], acc)
            dve.wait_ge(mix_done["gat2"], 1)
            dve.wait_ge(state["gat1"], 1)
            link(v.tensor_tensor(xs["y"][:, :], acc, xs["in"][:, :], ALU.add))
            norm("n2", state["r8a"], xs["in"])
            t_copy("r8a", R8)
            relu("r8a", state["r8b"], acc2)
            t_copy("r8b", R8)
            dve.wait_ge(used, last_of("r8b"))
            dve.wait_ge(state["r8a"], 1)
            link(v.tensor_tensor(xs["y"][:, :], acc, xs["in"][:, :], ALU.add))
            norm("n3", result, xs["y"])


def kernel(**inputs):
    import concourse.bacc as bacc
    from concourse.bass_utils import run_bass_kernel_spmd

    get = {k: np.asarray(v) for k, v in inputs.items()}

    def chunked(w):
        return w.reshape(KC, P, -1).transpose(1, 0, 2).reshape(P, -1)

    mats = {"root1": get["L0_gnn_W_root1"], "root2": get["L0_gnn_W_root2"],
            "Wg_h": get["L0_gnn_Wg"][:, :D].T, "Wg_q": get["L0_gnn_Wg"][:, D:].T,
            "Wq_h": get["L0_gnn_Wq"][:, :D].T, "Wq_q": get["L0_gnn_Wq"][:, D:].T,
            "gcn1": get["L1_gnn_W1"], "gcn2": get["L1_gnn_W2"], "gat1": get["L2_gnn_W1"], "gat2": get["L2_gnn_W2"],
            "r8a_root": get["L3_gnn_root1"], "r8b_root": get["L3_gnn_root2"]}
    for r in range(R3):
        mats[f"rel1_{r}"], mats[f"rel2_{r}"] = get["L0_gnn_W_rel1"][r], get["L0_gnn_W_rel2"][r]
    for r in range(R8):
        mats[f"r8a_{r}"], mats[f"r8b_{r}"] = get["L3_gnn_W1"][r], get["L3_gnn_W2"][r]
    query = get["L0_gnn_query_embs"]
    biases = [get[k.replace("_", "_gnn_")] for k in BIAS]
    att = [get[k] for k in ("L2_gnn_att_src1", "L2_gnn_att_dst1", "L2_gnn_att_src2", "L2_gnn_att_dst2")]
    edges = np.stack([get[k].reshape(EP, ET) for k in ("src", "dst", "edge_type_3", "edge_type_8")], 1)
    arrays = {
        "x": get["x"],
        "edges": edges,
        "consts": constants(),
        "consts16": bf16_constants(),
        "picks": bias_picks(),
        "biases": np.stack(biases),
        "query_t": query.reshape(B // 2, P, KC, P).transpose(3, 0, 2, 1).reshape(P, -1),
        "query": np.ascontiguousarray(query.transpose(1, 0, 2)),
        "att": np.stack(att),
        "weights": np.stack([chunked(mats[n]) for n in NAMES]),
    }
    arrays = {k: np.ascontiguousarray(v) for k, v in arrays.items()}
    nc = bacc.Bacc("TRN2", target_bir_lowering=False, num_devices=1)
    args = [nc.dram_tensor(f"in_{k}", a.shape, mybir.dt.from_np(a.dtype), kind="ExternalInput").ap() for k, a in arrays.items()]
    out = nc.dram_tensor("out", (N, D), F32, kind="ExternalOutput").ap()
    build(nc, *args, out)
    r = run_bass_kernel_spmd(nc, [{f"in_{k}": a for k, a in arrays.items()}], core_ids=[0])
    return r.results[0]["out"]
```

```python
from contextlib import ExitStack

import concourse.bass as bass
import numpy as np
from concourse import mybir

F32 = mybir.dt.float32
BF16 = mybir.dt.bfloat16
I32 = mybir.dt.int32
ALU = mybir.AluOpType
ACT = mybir.ActivationFunctionType
AX = mybir.AxisListType

P = 128
N = 64
D = 768
HD = D // 2
KC = D // P
E = 2112
FULL = E // P
REST = E - FULL * P
ET = FULL + 1
B, L = 8, 64
NB = N // B
TILES = N // 2
EPS = 1e-5
SLOPE = 0.2
R3, R8 = 3, 8
MAT = KC * D
FAR = 3e38

NAMES = (["rel1_0", "rel1_1", "rel1_2", "root1", "rel2_0", "rel2_1", "rel2_2", "root2",
          "Wg_h", "Wg_q", "Wq_h", "Wq_q", "gcn1", "gcn2", "gat1", "gat2"]
         + [f"r8a_{r}" for r in range(R8)] + ["r8a_root"] + [f"r8b_{r}" for r in range(R8)] + ["r8b_root"])
LOADS = (["Q", "Wg_q", "rel1_0", "rel1_1", "rel1_2", "root1", "Wg_h", "Wq_h", "Wq_q",
          "rel2_0", "rel2_1", "rel2_2", "root2", "Wg_h", "Wq_h", "Wq_q", "gcn1", "gcn2", "gat1", "gat2"]
         + [f"r8a_{r}" for r in range(R8)] + ["r8a_root"] + [f"r8b_{r}" for r in range(R8)] + ["r8b_root"])
GB = 3
WGQ_PARTS = 3
FIRST_SLOTS = 5
GATE_SLOTS = 3
ALL_SLOTS = FIRST_SLOTS + GATE_SLOTS + 1
WIDE_FROM = LOADS.index("gat2")

BIAS = ["L0_b1", "L0_b2", "L0_bq", "L1_b1", "L1_b2", "L2_b1", "L2_b2", "L3_b1", "L3_b2", "L0_bg"]

C_EYE = 0
C_SUM = C_EYE + N
C_AVG = C_SUM + 2 * N - 2
C_DIF = C_AVG + P
C_PAIR = C_DIF + P
C_MEAN = C_PAIR + P
C_ONE = C_MEAN + P
C_ID = C_ONE + P
C_END = C_ID + P
Q_TILES = TILES // B
S_EYE = 0
S_SEL = S_EYE + P
S_GATHER = S_SEL + Q_TILES * P
G_WIDTH = P + 2 * NB
S_END = S_GATHER + 4 * G_WIDTH
BF16_ONE = 0x3F80


def constants():
    c = np.zeros((P, C_END), np.float32)
    p = np.arange(P)
    same = (p[:, None] % N == p[None, :] % N).astype(np.float32)
    c[:, C_EYE:C_EYE + N] = same[:, :N]
    c[:N, C_SUM + N - 2] = 1
    c[N:, C_SUM + N - 1] = 1
    c[:, C_AVG:C_AVG + P] = same / 2
    c[:, C_DIF:C_DIF + P] = np.eye(P, dtype=np.float32) - same / 2
    c[:, C_PAIR:C_PAIR + P] = same
    c[:, C_MEAN:C_MEAN + P] = same / D
    c[:, C_ONE:C_ONE + P] = 1
    c[:, C_ID:C_ID + P] = np.eye(P, dtype=np.float32)
    return c


def bf16_constants():
    s = np.zeros((P, S_END), np.uint16)
    one = np.uint16(BF16_ONE)
    p = np.arange(P)
    s[:, S_EYE:S_EYE + P][p[:, None] % N == p[None, :] % N] = one
    for k in range(Q_TILES):
        for i in range(2):
            col = S_SEL + k * P + i * N
            s[np.arange(N), col + np.arange(N)] = one
            for part in range(3):
                s[N + NB * part + 2 * k + i, col:col + N] = one
    for g in range(2):
        for h in range(2):
            col = S_GATHER + (2 * g + h) * G_WIDTH + 2 * NB
            for j in range(4):
                for n in range(NB):
                    s[h * N + (4 * g + j) * NB + n, col + 32 * j + n] = one
    return s


def bias_picks():
    c = np.zeros((len(BIAS), len(BIAS) * N), np.float32)
    for i in range(len(BIAS)):
        c[i, i * N:(i + 1) * N] = 1
    return c


def ring():
    slots, held, uses, out = [], {}, {}, []
    for i in range(len(LOADS)):
        if i < WIDE_FROM:
            s = i % FIRST_SLOTS
        elif i < WIDE_FROM + ALL_SLOTS - FIRST_SLOTS:
            s = FIRST_SLOTS + i - WIDE_FROM
        else:
            s = slots[i - ALL_SLOTS]
        slots.append(s)
        uses[s] = uses.get(s, 0) + (i >= 2)
        out.append((s, uses[s], held.get(s)))
        held[s] = i
    return out


RING = ring()
KEEP_START = 14
KEEP_ALPHA, KEEP_NORM, KEEP_NORM_BIAS, KEEP_PARTS, KEEP_EXP, KEEP_RELU = 6, 4, 1, 4, 13, 2
CHUNKS = [h * KC // 2 + k for k in range(KC // 2) for h in range(2)]
VAR_AT = 3
LATE = 2
FIRST, LAST = slice(0, P), slice(P, HD)
TURNS = ["rgcn1", "g1_h", "g1_q", "rgcn2", "g2_h", "g2_q", "gcn1", "gcn2", "gat1", "gat2", "r8a", "r8a_x", "r8b"]
CONVS = ["rgcn1", "rgcn2", "gcn1", "gcn2", "gat1", "gat2", "r8a", "r8b"]


def build(nc, x, edges, edges_rest, consts, consts16, picks, biases, query_t, query, att, weights, out):
    with ExitStack() as ctx:
        def sb(name, shape, dt=F32):
            return ctx.enter_context(nc.sbuf_tensor(name, shape, dt))

        def sem(name):
            return ctx.enter_context(nc.semaphore(name))

        def sems(what, names):
            return {n: sem(f"{what}_{n}") for n in names}

        ps_t = ctx.enter_context(nc.psum_tensor("ps_t", [P, 2, 512], F32))
        ps_xa = ctx.enter_context(nc.psum_tensor("ps_xa", [P, 2, 512], F32))
        ps_x, ps_acc = ps_xa[:, 0, :], ps_xa[:, 1, :]
        ps_g = ctx.enter_context(nc.psum_tensor("ps_g", [P, 4, 512], F32))
        ps_qi = ps_t[:, :, 0:HD // 2]
        ps_s = ps_t[:, 1, :]
        acc, acc2 = ps_acc[:, 0:HD], ps_t[:, 0, 0:HD]
        acc_alpha = ps_x[:, 0:HD]
        keep = ps_g[:, 3, 0:HD]

        def early_ps(turn):
            return (ps_acc if turn in ("g1_q", "rgcn2", "g2_q") else ps_x)[:, 0:LATE * N]

        def late_ps(turn):
            return (ps_t[:, 1, :] if turn in ("rgcn1", "r8a_x") else ps_g[:, 3, :])[:, 0:(KC - LATE) * N]

        w_ring = sb("w_ring", [P, FIRST_SLOTS, MAT])
        gatebuf = sb("gatebuf", [P, GATE_SLOTS, MAT])
        flat = gatebuf[:, :, :].rearrange("p a b -> p (a b)")
        by_batch = flat.rearrange("p (g s i f) -> p g s i f", g=GATE_SLOTS, s=2, i=GB)
        by_batch16 = flat.bitcast(BF16).rearrange("p (g s i f) -> p g s i f", g=GATE_SLOTS, s=2, i=GB)

        def q_rows(b):
            return by_batch[:, b // GB, 0, b % GB, :]

        def qg_hm(b):
            return by_batch16[:, b // GB, 1, b % GB, 0:D]

        def lows(b):
            return by_batch16[:, b // GB, 1, b % GB, D:2 * D]

        work = sb("work", [P, 4 * HD + MAT])
        y_s = work[:, 0:4 * HD].rearrange("p (s h f) -> p s h f", s=2, h=2)
        att_s = work[:, 4 * D:6 * D].rearrange("p (t f) -> p t f", t=2)
        prod = work[:, 6 * D:8 * D].rearrange("p (t f) -> p t f", t=2)
        hot8 = work[:, 0:ET * R8 * N // 2].bitcast(BF16).rearrange("p (t k) -> p t k", t=ET)
        hot3 = flat[:, 0:ET * R3 * N // 2].bitcast(BF16).rearrange("p (t k) -> p t k", t=ET)
        att_rows = sb("att_rows", [P, 4, HD])
        hot_src = att_rows[:, :, :].rearrange("p a b -> p (a b)")[:, 0:ET * P // 2].bitcast(BF16).rearrange("p (t k) -> p t k", t=ET)
        cst = sb("cst", [P, C_END])
        cst16 = sb("cst16", [P, S_END], mybir.dt.uint16)
        bias_sel = sb("bias_sel", [len(BIAS), len(BIAS) * N])
        bias_rows = sb("bias_rows", [len(BIAS), D])
        iota = flat[:, MAT:MAT + R8 * N]
        iota_i = flat[:, MAT + R8 * N:MAT + 2 * R8 * N].bitcast(I32)
        edges_i = sb("edges_i", [P, 4, FULL], I32)
        rest_i = sb("rest_i", [REST, 4], I32)
        edges_f = sb("edges_f", [P, 4, ET])
        keys = sb("keys", [P, 2, ET])
        a3 = sb("a3", [P, 3, N])
        a8 = sb("a8", [P, R8 * N])
        cnt8 = work[:, ET * R8 * N // 2:ET * R8 * N // 2 + R8 * N]
        c_sd = sb("c_sd", [P, 2, N])
        c_ds = sb("c_ds", [P, N])
        far = sb("far", [P, N])
        mask = sb("mask", [P, N])
        dinv_row = sb("dinv_row", [P, N])
        dinv_col = sb("dinv_col", [P, 1])
        deg = sb("deg", [P, 1])
        xs = {n: sb(f"x_{n}", [P, HD]) for n in ("in", "a", "b", "y")}
        cnt3, raw3 = xs["b"][:, 0:R3 * N], xs["b"][:, R3 * N:2 * R3 * N]
        x_low = sb("x_low", [P, HD])
        parts = by_batch16[:, GATE_SLOTS - 1, 0, GB - 1, :]
        high = parts[:, 0:2 * HD].rearrange("p (t f) -> p t f", t=2)
        mid, low = parts[:, 2 * HD:3 * HD], parts[:, 3 * HD:4 * HD]
        th = x_low
        qi = sb("qi", [P, HD])
        alpha = xs["b"]
        warm = x_low[:, :].bitcast(BF16)
        xt = sb("xt", [P, KC * N])
        qit = sb("qit", [P, KC * N])
        stat = sb("stat", [P, 6])
        mv = sb("mv", [P, 2])
        st = sb("st", [P, 8])
        a_part = sb("a_part", [P, 2])
        diag = sb("diag", [P, N])
        e_t = sb("e_t", [P, 5, N])
        al_t = sb("al_t", [P, 2, N])
        power = sb("power", [P, N])
        table = sb("table", [P, 1])

        identity = cst[:, C_ID:C_ID + P]
        eye, one = cst[:, C_EYE:C_EYE + N], cst[:, C_ONE:C_ONE + P]

        def bias_pick(i):
            return bias_sel[:, i * N:(i + 1) * N]

        bits = cst16[:, :].bitcast(BF16)
        eye_b = bits[:, S_EYE:S_EYE + P]

        def sel(k):
            return bits[0:N + 32, S_SEL + k * P:S_SEL + (k + 1) * P]

        def gather(g, h, part):
            at = S_GATHER + (2 * g + h) * G_WIDTH + 2 * NB - NB * part
            return bits[:, at:at + P]

        def last_of(name):
            return {"hg_g1": 7, "al_g1": 9, "hg_g2": 14, "al_g2": 16, "gcn1": 17, "gcn2": 18, "gat1": 19, "gat2": 20}[name]

        first_load = {"rgcn1": 2, "rgcn2": 9, "r8a": 20, "r8b": 20 + R8 + 1}

        def slot(i):
            s = RING[i][0]
            if s == ALL_SLOTS - 1:
                return work[:, 4 * HD:]
            return w_ring[:, s, :] if s < FIRST_SLOTS else gatebuf[:, s - FIRST_SLOTS, :]

        def gathered_rows(b):
            return (lows(b)[N:N + 32, :].rearrange("p (h f) -> p h f", h=2),
                    (ps_t if b < 4 else ps_g[:, 2:4, :])[32 * (b % 4):32 * (b % 4) + 32, :, 0:HD])

        def qi_quarter(h, group, part):
            q = 2 * h + part
            r = h * N + 32 * group
            return qi[r:r + 32, part * HD // 2:(part + 1) * HD // 2], ps_qi[32 * q:32 * q + 32, group, :]

        const_in, edges_in, x_in, bias_in, att_in = (sem(n) for n in ("const_in", "edges_in", "x_in", "bias_in", "att_in"))
        query_in = [sem(f"query_in_{g}") for g in range(GATE_SLOTS)]
        query_doubled, out_done = sem("query_doubled"), sem("out_done")
        loaded = [sem(f"loaded_{s}") for s in range(ALL_SLOTS)]
        used = sem("weights_used")
        vec = sem("vec_chain")
        hot3_ready, hot8_ready = sem("hot3_ready"), sem("hot8_ready")
        counts3, counts8 = sem("counts3"), sem("counts8")
        a3_copied, a8_copied = sem("a3_copied"), sem("a8_copied")
        cnt3_ps, cnt8_ps, a3_ready, a8_ready = (sem(n) for n in ("cnt3_ps", "cnt8_ps", "a3_ready", "a8_ready"))
        csd_ready, cds_ps, deg_ready = sem("csd_ready"), sem("cds_ps"), sem("deg_ready")
        q_in = [sem(f"q_in_{k}") for k in range(B // 2)]
        wgq_in = [[sem(f"wgq_in_{h}{part}") for part in range(WGQ_PARTS)] for h in range(2)]
        qg_ps, qg_high, qg_read, qg_split = sem("qg_ps"), sem("qg_high"), sem("qg_read"), sem("qg_split")
        qg_mid, qg_placed = sem("qg_mid"), sem("qg_placed")
        const16_in = sem("const16_in")
        state = sems("state", CONVS[1:])
        xt_done, xt_early, xt_late = sem("xt_done"), sem("xt_early"), sem("xt_late")
        relational = ["rgcn1", "rgcn2", "r8a", "r8b"]
        y_done, y_v, y_a, y_used, summed = (sems(n, relational) for n in ("y_done", "y_v", "y_a", "y_used", "summed"))
        gates = ["g1", "g2"]
        h_ready, hg_high, hg_split = (sems(n, gates) for n in ("h_ready", "hg_high", "hg_split"))
        gathered, rows_v, rows_a = (sems(n, gates) for n in ("gathered", "rows_v", "rows_a"))
        qi_v, qi_a = sems("qi_v", gates), sems("qi_a", gates)
        tile_sum, tile_sig, tile_prod, tile_red = (sems(n, gates) for n in ("tile_sum", "tile_sig", "tile_prod", "tile_red"))
        tanh_done, al_done = (sems(n, gates) for n in ("tanh_done", "al_done"))
        sum_ready, mean_ps, square_ready, square_ps, var_ready, rstd_ready = (
            sem(n) for n in ("sum_ready", "mean_ps", "square_ready", "square_ps", "var_ready", "rstd_ready"))
        mv_ready, mv_ps, x_ready = (sem(n) for n in ("mv_ready", "mv_ps", "x_ready"))
        warm_set = sem("warm_set")
        zeros_set, gcn_copied, gcn_summed = sem("zeros_set"), sem("gcn_copied"), sem("gcn_summed")
        dinv_ready, power_set, iota_made, a3_zeros = (sem(n) for n in ("dinv_ready", "power_set", "iota_made", "a3_zeros"))
        gats = ["gat1", "gat2"]
        terms, diag_ready, h_copied = (sems(n, gats) for n in ("terms", "diag_ready", "h_copied"))
        logits_ps, exp_in, exp_done, alpha_ready, alphat_ps, alphat_ready, mix_done = (
            sems(n, gats) for n in ("logits_ps", "exp_in", "exp_done", "alpha_ready", "alphat_ps", "alphat_ready", "mix_done"))
        result = sem("result")

        block = ctx.enter_context(nc.Block())

        @block.sync
        def _(sp):
            sp.dma_start(edges_i[:, :, :], edges).then_inc(edges_in, 16)
            sp.dma_start(rest_i[:, :], edges_rest).then_inc(edges_in, 16)

            def load(i):
                s, _, before = RING[i]
                if before is not None:
                    sp.wait_ge(used, before + 1)
                sp.dma_start(slot(i), weights[NAMES.index(LOADS[i])]).then_inc(loaded[s], 16)

            wq, wq_from = (a.rearrange("p (c n) -> p c n", c=KC) for a in (slot(1), weights[NAMES.index("Wg_q")]))
            for k in range(B // 2):
                rows = slice(k * D, (k + 1) * D)
                sp.dma_start(slot(0)[:, rows], query_t[:, rows]).then_inc(q_in[k], 16)
                if k < 2:
                    for part in range(WGQ_PARTS):
                        at = slice(part * KC // WGQ_PARTS, (part + 1) * KC // WGQ_PARTS), slice(k * HD, (k + 1) * HD)
                        sp.dma_start(wq[:, *at], wq_from[:, *at]).then_inc(wgq_in[k][part], 16)
                if k == 0:
                    sp.dma_start(cst[:, :], consts).then_inc(const_in, 16)
            sp.dma_start(bias_rows[:, :], biases).then_inc(bias_in, 16)
            sp.dma_start(bias_sel[:, :], picks).then_inc(bias_in, 16)
            sp.dma_start(cst16[:, :], consts16).then_inc(const16_in, 16)
            for h in range(2):
                sp.dma_start(xs["in"][h * N:(h + 1) * N, :], x[:, h * HD:(h + 1) * HD]).then_inc(x_in, 16)
            for i in range(2, FIRST_SLOTS):
                load(i)
            sp.wait_ge(counts3, 1)
            sp.wait_ge(hot8_ready, 2)
            for g, first in enumerate(range(0, B, GB)):
                n = min(GB, B - first)
                sp.dma_start(by_batch[0:N, g, 0, 0:n, :], query[:, first:first + n, :]).then_inc(query_in[g], 16)
            sp.wait_ge(counts8, 1)
            for k in range(4):
                for h in range(2):
                    sp.dma_start(att_rows[h * N:(h + 1) * N, k, :],
                                 att[k:k + 1, h * HD:(h + 1) * HD].to_broadcast([N, HD])).then_inc(att_in, 16)
            for i in range(FIRST_SLOTS, len(LOADS)):
                if 0 <= i - WIDE_FROM < ALL_SLOTS - FIRST_SLOTS:
                    sp.wait_ge(tile_red["g2"], min(TILES, GB * (i - WIDE_FROM + 1) * Q_TILES))
                load(i)
            sp.wait_ge(result, 1)
            for h in range(2):
                sp.dma_start(out[:, h * HD:(h + 1) * HD], xs["y"][h * N:(h + 1) * N, :]).then_inc(out_done, 16)
            sp.wait_ge(out_done, 32)

        @block.gpsimd
        def _(pool):
            nc.gpsimd.iota(iota_i, [[1, R8 * N]], base=0, channel_multiplier=0).then_inc(iota_made, 1)
            nc.gpsimd.memset(power[:, :], -0.5).then_inc(power_set, 1)
            pool.wait_ge(power_set, 1)
            for half in range(2):
                nc.gpsimd.memset(a3[half * N:(half + 1) * N, 2 - half, :], 0.0).then_inc(a3_zeros, 1)
                pool.wait_ge(a3_zeros, half + 1)
            nc.gpsimd.memset(al_t[:, :, :], 0.0).then_inc(zeros_set, 1)
            pool.wait_ge(zeros_set, 1)
            pool.wait_ge(deg_ready, 1)
            nc.gpsimd.tensor_tensor(dinv_col[:, :], deg[:, :], power[:, 0:1], ALU.pow).then_inc(dinv_ready, 1)
            pool.wait_ge(dinv_ready, 1)
            nc.gpsimd.tensor_tensor(dinv_row[:, :], dinv_row[:, :], power[:, :], ALU.pow).then_inc(dinv_ready, 1)
            pool.wait_ge(dinv_ready, 2)
            for n in range(4):
                pool.wait_ge(var_ready, n + 1)
                nc.gpsimd.tensor_tensor(st[:, 4:5], st[:, 3:4], power[:, 0:1], ALU.pow).then_inc(rstd_ready, 1)

        @block.tensor
        def _(pe):
            mm = nc.tensor.matmul

            def weights_of(i):
                pe.wait_ge(loaded[RING[i][0]], 16 * RING[i][1])
                return slot(i).rearrange("p (c n) -> p c n", c=KC)

            def bias(name, to):
                i = BIAS.index(name)
                for h in range(2):
                    mm(to[h * N:(h + 1) * N, :], bias_pick(i), bias_rows[:, h * HD:(h + 1) * HD],
                       start=True, stop=False)

            def keep_clock(n):
                for _ in range(n):
                    mm(keep, eye_b, bits[:, 0:HD], start=True, stop=True)

            def step_w(i, lhs, start, stop, to, chunks=range(KC), turn=None):
                w = weights_of(i)
                for k in chunks:
                    if turn and k in (0, LATE):
                        pe.wait_ge(xt_late if k else xt_early, TURNS.index(turn) + 1)
                    for h in range(2):
                        ins = mm(to[h * N:(h + 1) * N, :], lhs[:, k * N:(k + 1) * N], w[:, CHUNKS[k], h * HD:(h + 1) * HD],
                                 start=start and k == 0, stop=stop and k == KC - 1)
                if k == KC - 1:
                    ins.then_inc(used, 1)

            def transposed(src, rhs, turn, *ready):
                for k in range(KC // 2):
                    if k < 2:
                        for s, before in ready:
                            pe.wait_ge(s, before + k + 1)
                    dst = early_ps(turn)[:, k * P:(k + 1) * P] if 2 * k < LATE else late_ps(turn)[:, (2 * k - LATE) * N:(2 * k + 2 - LATE) * N]
                    if rhs is None:
                        ins = nc.tensor.transpose(dst, src[:, k * P:(k + 1) * P], identity)
                    else:
                        ins = mm(dst, src[:, k * P:(k + 1) * P], rhs, start=True, stop=True)
                    if 2 * k + 2 in (LATE, KC):
                        ins.then_inc(xt_done, 1)

            wq = slot(1).rearrange("p (c n) -> p c n", c=KC)
            qt = slot(0)[:, 0:KC * B * L].rearrange("p (k c r) -> p k c r", k=B // 2, c=KC)

            def query_block(h, k):
                m = h * (B // 2) + k
                if h == 0:
                    pe.wait_ge(q_in[k], 16)
                if m >= 4:
                    pe.wait_ge(qg_read, m - 3)
                dst = ps_g[:, m % 4, 0:HD]
                for c in range(KC):
                    if k == 0 and c % (KC // WGQ_PARTS) == 0:
                        pe.wait_ge(wgq_in[h][c * WGQ_PARTS // KC], 16)
                    ins = mm(dst, qt[:, k, c, :], wq[:, c, h * HD:(h + 1) * HD], start=c == 0, stop=c == KC - 1)
                if m == B - 1:
                    ins.then_inc(used, 2)
                else:
                    ins.then_inc(qg_ps, 1)

            pe.wait_ge(warm_set, 1)
            for _ in range(KEEP_START):
                mm(keep, warm[:, 0:P], warm[:, 0:HD], start=True, stop=True)
            query_block(0, 0)
            query_block(0, 1)
            pe.wait_ge(hot3_ready, 2)
            for t in range(ET):
                ins = mm(ps_t[:, 0, 0:R3 * N], hot_src[:, t, :], hot3[:, t, :], start=t == 0, stop=t == ET - 1)
            ins.then_inc(counts3, 1)
            query_block(0, 2)
            query_block(0, 3)
            pe.wait_ge(const_in, 16)
            pe.wait_ge(a3_copied, 1)
            mm(ps_t[:, 1, 0:R3 * N], one[0:N, :], raw3[0:N, :], start=True, stop=True).then_inc(cnt3_ps, 1)
            pe.wait_ge(csd_ready, 1)
            mm(ps_x[:, 0:N], c_sd[0:N, :, :].rearrange("p a n -> p (a n)"), eye[0:N, :], start=True, stop=True)
            mm(ps_x[:, N:2 * N], one[0:N, :], c_sd[0:N, 0, :], start=True, stop=True).then_inc(cds_ps, 1)
            for k in range(3):
                query_block(1, k)
            pe.wait_ge(hot8_ready, 2)
            for t in range(ET):
                ins = mm(ps_t[:, 0, :], hot_src[:, t, :], hot8[:, t, :], start=t == 0, stop=t == ET - 1)
            ins.then_inc(counts8, 1)
            pe.wait_ge(x_in, 32)
            pe.wait_ge(deg_ready, 1)
            pe.wait_ge(a3_ready, 4)
            transposed(xs["in"], None, "rgcn1")
            query_block(1, 3)
            pe.wait_ge(a8_copied, 1)
            mm(ps_acc[:, :], one[0:N, :], a8[0:N, :], start=True, stop=True).then_inc(cnt8_ps, 1)
            pe.wait_ge(bias_in, 32)
            bias("L0_b1", acc2)

            def gcn1(load):
                transposed(xs["y"], None, "gcn1", (state["gcn1"], 0))
                step_w(load, xt, True, False, acc, range(VAR_AT), "gcn1")
                variance(0)
                step_w(load, xt, False, True, acc, range(VAR_AT, KC), "gcn1")
                pe.wait_ge(gcn_copied, 1)
                for h in range(2):
                    ins = mm(acc2[h * N:(h + 1) * N, :], al_t[:, h, :], y_s[:, 0, 0, :], start=False, stop=True)
                ins.then_inc(gcn_summed, 1)

            def gcn2(load):
                transposed(xs["a"], al_t[:, :, :].rearrange("p h n -> p (h n)"), "gcn2", (state["gcn2"], 0))
                step_w(load, xt, False, True, acc, turn="gcn2")

            def conv(name, load, src, adj, odd, rels, to):
                if name != "rgcn1":
                    transposed(src, None, name, (state[name], 0))
                pairs = rels // 2
                steps = pairs + rels % 2

                def times_w(p):
                    if p >= 2:
                        pe.wait_ge(y_v[name], p - 1)
                        pe.wait_ge(y_a[name], p - 1)
                    ws = [weights_of(load + 2 * p + r) for r in range(2)]
                    for h in range(2):
                        for k in range(KC):
                            if p == 0 and h == 0 and k in (0, LATE):
                                pe.wait_ge(xt_late if k else xt_early, TURNS.index(name) + 1)
                            for r in range(2):
                                ins = mm(ps_g[r * N:(r + 1) * N, 2 * (p % 2) + h, 0:HD], xt[:, k * N:(k + 1) * N],
                                         ws[r][:, CHUNKS[k], h * HD:(h + 1) * HD], start=k == 0, stop=k == KC - 1)
                        ins.then_inc(*((used, 2) if h else (y_done[name], 1)))
                        if name == "r8a" and p == 0 and h == 0:
                            variance(2)

                def times_a(p):
                    pe.wait_ge(y_v[name], p + 1)
                    if p < pairs:
                        pe.wait_ge(y_a[name], p + 1)
                    for h in range(2):
                        rhs = y_s[:, p % 2, h, :] if p < pairs else y_s[:, p % 2, 0, :]
                        ins = mm(to[h * N:(h + 1) * N, :], adj(p) if p < pairs else odd(h), rhs,
                                 start=False, stop=p == steps - 1)
                    ins.then_inc(summed[name] if p == steps - 1 else y_used[name], 1)

                for p in range(pairs):
                    times_w(p)
                    if name == "r8a" and p == 1:
                        pe.wait_ge(x_ready, 3)
                        transposed(xs["in"], None, "r8a_x")
                    if p:
                        times_a(p - 1)
                if rels % 2:
                    step_w(load + 2 * pairs, xt, True, True, ps_g[:, 2 * (pairs % 2), 0:HD])
                    times_a(pairs - 1)
                if name == "r8a":
                    step_w(load + rels, qit, False, False, to, turn="r8a_x")
                else:
                    step_w(load + rels, xt, False, False, to)
                times_a(steps - 1)

            def gate(g, load):
                if g == "g1":
                    pe.wait_ge(a8_ready, 2)
                bias("L0_bg", acc)
                transposed(xs["a"], None, f"{g}_h", (h_ready[g], 0))
                step_w(load, xt, False, True, acc, turn=f"{g}_h")

                def alpha_of_h(chunks):
                    step_w(load + 1, xt, False, False, acc_alpha, chunks)

                bias("L0_bq", acc_alpha)
                alpha_of_h(range(0, 2))
                pe.wait_ge(const16_in, 16)
                for i in range(2):
                    for h in range(2):
                        for part, src in enumerate((high[:, 0, :], mid, low)):
                            if i == 0 and h == 0:
                                pe.wait_ge(*((hg_high[g], 1), (hg_split[g], 1), (hg_split[g], 2))[part])
                            ins = mm((ps_t[:, h, 0:HD] if i == 0 else ps_g[:, 2 + h, 0:HD]), gather(i, h, part), src,
                                     start=part == 0, stop=part == 2)
                    ins.then_inc(gathered[g], 1)
                pe.wait_ge(qg_split, B)
                pe.wait_ge(qg_placed, 4 * B)

                def add(t):
                    b = t // Q_TILES
                    if t % Q_TILES == 0:
                        pe.wait_ge(rows_a[g] if b % 2 else rows_v[g], b // 2 + 1)
                    if t >= 2:
                        pe.wait_ge(tile_sig[g], t - 1)
                    if t == 1:
                        alpha_of_h(range(2, 4))
                        pe.wait_ge(rows_v[g], B // 2)
                        pe.wait_ge(rows_a[g], B // 2)
                    for h in range(2):
                        dst = ps_g[:, 2 * (t % 2) + h, 0:HD]
                        mm(dst, eye_b, qg_hm(b)[:, h * HD:(h + 1) * HD], start=True, stop=False)
                        ins = mm(dst, sel(t % Q_TILES), lows(b)[0:N + 32, h * HD:(h + 1) * HD], start=False, stop=True)
                    ins.then_inc(tile_sum[g], 1)

                def reduce(t):
                    pe.wait_ge(tile_prod[g], t + 1)
                    if t == 0:
                        pe.wait_ge(rows_v[g], 2)
                        pe.wait_ge(rows_a[g], 2)
                    half = TILES // 2
                    w0 = C_SUM + N - 2 - 2 * (t % half)
                    for q in range(4):
                        ins = mm(ps_qi[32 * q:32 * q + 32, t // half, :], cst[:, w0:w0 + 32],
                                 prod[:, t % 2, q * HD // 2:(q + 1) * HD // 2],
                                 start=t % half == 0, stop=t % half == half - 1)
                    ins.then_inc(tile_red[g], 1)

                for t in range(TILES + 2):
                    if t < TILES:
                        add(t)
                    if t >= 2:
                        reduce(t - 2)
                    if t == TILES:
                        alpha_of_h(range(4, KC))
                pe.wait_ge(qi_v[g], 2)
                pe.wait_ge(qi_a[g], 2)
                bias("L0_b2" if g == "g1" else "L1_b1", acc2)
                transposed(qi, None, f"{g}_q", (qi_v[g], 2), (qi_a[g], 2))
                step_w(load + 2, qit, False, True, acc_alpha, turn=f"{g}_q")

            def mean(n):
                pe.wait_ge(sum_ready, n + 1)
                mm(ps_s[:, 0:1], cst[:, C_MEAN:C_MEAN + P], st[:, 0:1], start=True, stop=True).then_inc(mean_ps, 1)

            def variance(n):
                pe.wait_ge(square_ready, n + 1)
                mm(ps_s[:, 1:2], cst[:, C_MEAN:C_MEAN + P], st[:, 1:2], start=True, stop=True).then_inc(square_ps, 1)

            def last_norm():
                pe.wait_ge(mv_ready, 1)
                mm(ps_s[:, 0:2], cst[:, C_AVG:C_AVG + P], mv[:, :], start=True, stop=True)
                mm(ps_s[:, 2:3], cst[:, C_DIF:C_DIF + P], mv[:, 0:1], start=True, stop=True).then_inc(mv_ps, 1)

            def attend(name):
                pe.wait_ge(diag_ready[name], 1)
                mm(ps_s[:, 0:N], one, diag[:, :], start=True, stop=True)
                pe.wait_ge(terms[name], 3 if name == "gat1" else 2)
                mm(ps_s[:, N:N + 1], cst[:, C_PAIR:C_PAIR + P], st[:, 6:7] if name == "gat1" else a_part[:, 1:2], start=True, stop=True).then_inc(logits_ps[name], 1)
                keep_clock(KEEP_EXP)
                pe.wait_ge(alpha_ready[name], 1)
                mm(ps_x[:, 0:N], e_t[0:N, 3:5, :].rearrange("p a n -> p (a n)"), eye[0:N, :],
                   start=True, stop=True).then_inc(alphat_ps[name], 1)
                pe.wait_ge(alphat_ready[name], 2)
                pe.wait_ge(h_copied[name], 1)
                for h in range(2):
                    ins = mm(acc[h * N:(h + 1) * N, :], al_t[:, h, :], qi[:, :], start=False, stop=True)
                ins.then_inc(mix_done[name], 1)
                if name == "gat1":
                    keep_clock(KEEP_RELU)

            def pair3(p):
                return a3[:, 0, :]

            def odd3(h):
                return a3[:, 1 + h, :]

            def pair8(p):
                return a8[:, 2 * p * N:(2 * p + 1) * N]

            load = 2
            pe.wait_ge(a3_zeros, 2)
            pe.wait_ge(qg_read, B)
            conv("rgcn1", load, xs["in"], pair3, odd3, R3, acc2)
            gate("g1", load + 4)
            load += 7
            keep_clock(KEEP_ALPHA)
            conv("rgcn2", load, xs["b"], pair3, odd3, R3, acc2)
            gate("g2", load + 4)
            load += 7
            keep_clock(KEEP_ALPHA + KEEP_NORM)
            mean(0)
            keep_clock(KEEP_NORM)
            gcn1(load)
            bias("L1_b2", acc)
            gcn2(load + 1)
            keep_clock(KEEP_NORM)
            mean(1)
            keep_clock(KEEP_NORM)
            for k, name in enumerate(gats):
                src = xs["y"] if k == 0 else xs["a"]
                transposed(src, None, name, (state[name], 0))
                step_w(load + 2 + k, xt, True, False, acc2, range(VAR_AT), name)
                if k == 0:
                    variance(1)
                step_w(load + 2 + k, xt, False, True, acc2, range(VAR_AT, KC), name)
                bias(f"L2_b{k + 1}", acc)
                keep_clock(KEEP_PARTS)
                attend(name)
            bias("L3_b1", acc2)
            keep_clock(KEEP_NORM_BIAS)
            mean(2)
            bias("L3_b2", acc)
            load += 4
            conv("r8a", load, xs["y"], pair8, None, R8, acc2)
            mm(acc, identity, xs["in"][:, :], start=False, stop=False)
            conv("r8b", load + 1 + R8, xs["a"], pair8, None, R8, acc)
            last_norm()

        @block.scalar
        def _(act):
            copy = nc.scalar.copy

            def t_copy(turn, to=xt):
                act.wait_ge(xt_done, 2 * TURNS.index(turn) + 2)
                copy(to[:, LATE * N:], late_ps(turn)).then_inc(xt_late, 1)

            act.wait_ge(power_set, 1)
            nc.scalar.activation(table[:, :], power[:, 0:1], ACT.Sigmoid)
            for m in range(B):
                if m == B - 1:
                    t_copy("rgcn1")
                if m < B - 1:
                    act.wait_ge(qg_ps, m + 1)
                else:
                    act.wait_ge(used, 2)
                if m >= 2:
                    act.wait_ge(qg_split, m - 1)
                copy(high[:, m % 2, :], ps_g[:, m % 4, 0:HD]).then_inc(qg_high, 1)
                h, k = m // (B // 2), m % (B // 2)
                cols = slice(h * HD, (h + 1) * HD)
                act.wait_ge(qg_high, m + 1)
                for hh in range(2):
                    r = slice(hh * N, (hh + 1) * N)
                    copy(qg_hm(2 * k + hh)[r, cols], high[r, m % 2, :]).then_inc(qg_placed, 1)
                act.wait_ge(qg_mid, m + 1)
                for hh in range(2):
                    r, other = slice(hh * N, (hh + 1) * N), slice((1 - hh) * N, (2 - hh) * N)
                    copy(qg_hm(2 * k + hh)[other, cols], mid[r, :]).then_inc(qg_placed, 1)

            def y_copy(name, rels):
                for p in range(rels // 2):
                    act.wait_ge(used, first_load[name] + 2 * p + 2)
                    if p >= 2:
                        act.wait_ge(y_used[name], p - 1)
                    dst, src = y_s[:, p % 2, 1, :], ps_g[:, 2 * (p % 2) + 1, 0:HD]
                    if name == "r8a":
                        act.wait_ge(rstd_ready, 3)
                        nc.scalar.activation(dst, src, ACT.Copy, scale=st[:, 4:5]).then_inc(y_a[name], 1)
                    else:
                        copy(dst, src).then_inc(y_a[name], 1)
                    if name == "r8a" and p == 1:
                        t_copy("r8a_x", qit)

            def double_query(g):
                act.wait_ge(query_in[g], 16)
                n = min(GB, B - g * GB)
                copy(by_batch[N:P, g, 0, 0:n, :], by_batch[0:N, g, 0, 0:n, :]).then_inc(query_doubled, 1)

            def gate(g):
                def gate_sums(group):
                    act.wait_ge(tile_red[g], (group + 1) * TILES // 2)
                    for part in range(2):
                        copy(*qi_quarter(1, group, part)).then_inc(qi_a[g], 1)

                t_copy(f"{g}_h")
                act.wait_ge(used, last_of(f"hg_{g}"))
                copy(high[:, 0, :], acc).then_inc(hg_high[g], 1)
                for b in range(1, B, 2):
                    act.wait_ge(gathered[g], b // 4 + 1)
                    copy(*gathered_rows(b)).then_inc(rows_a[g], 1)
                for t in range(TILES):
                    if t == TILES // 2 + 3:
                        gate_sums(0)
                    act.wait_ge(tile_sum[g], t + 1)
                    if t >= 2:
                        act.wait_ge(tile_prod[g], t - 1)
                    nc.scalar.activation(att_s[:, t % 2, :].rearrange("p (h f) -> p h f", h=2),
                                         ps_g[:, 2 * (t % 2):2 * (t % 2) + 2, 0:HD], ACT.Sigmoid).then_inc(tile_sig[g], 1)
                gate_sums(1)
                act.wait_ge(qi_v[g], 4)
                act.wait_ge(qi_a[g], 4)
                nc.scalar.activation(th[:, :], qi[:, :], ACT.Tanh).then_inc(tanh_done[g], 1)
                t_copy(f"{g}_q", qit)
                act.wait_ge(used, last_of(f"al_{g}"))
                for cols in (FIRST, LAST):
                    nc.scalar.activation(alpha[:, cols], acc_alpha[:, cols], ACT.Sigmoid).then_inc(al_done[g], 1)

            double_query(0)
            double_query(1)
            y_copy("rgcn1", R3)
            double_query(2)
            gate("g1")
            t_copy("rgcn2")
            y_copy("rgcn2", R3)
            gate("g2")
            t_copy("gcn1")
            t_copy("gcn2")
            for name in gats:
                t_copy(name)
                act.wait_ge(exp_in[name], 1)
                nc.scalar.activation(e_t[:, 1, :], e_t[:, 0, :], ACT.Exp, bias=st[:, 7:8], scale=-1.0).then_inc(exp_done[name], 1)
                act.wait_ge(alphat_ps[name], 1)
                copy(al_t[N:P, 1, :], ps_x[N:P, 0:N]).then_inc(alphat_ready[name], 1)
            t_copy("r8a")
            y_copy("r8a", R8)
            t_copy("r8b")
            y_copy("r8b", R8)

        @block.vector
        def _(dve):
            v = nc.vector
            made = [0]

            def link(ins):
                made[0] += 1
                ins.then_inc(vec, 1)
                dve.wait_ge(vec, made[0])

            def tell(ins, s, value=1):
                ins.then_inc(s, 1)
                dve.wait_ge(s, value)

            f_src, f_dst, f_t3, f_t8 = (edges_f[:, k, :] for k in range(4))

            v.memset(warm, 0.0).then_inc(warm_set, 1)
            v.memset(edges_f[REST:P, :, FULL], -1.0)
            dve.wait_ge(edges_in, 32)
            v.tensor_copy(edges_f[0:REST, :, FULL], rest_i[:, :])
            link(v.tensor_copy(edges_f[:, :, 0:FULL], edges_i[:, :, :]))
            dve.wait_ge(iota_made, 1)
            link(v.tensor_copy(iota, iota_i))
            link(v.scalar_tensor_tensor(out=keys[:, 0, :], in0=f_t3, scalar=float(N), in1=f_dst, op0=ALU.mult, op1=ALU.add))
            link(v.scalar_tensor_tensor(out=keys[:, 1, :], in0=f_t8, scalar=float(N), in1=f_dst, op0=ALU.mult, op1=ALU.add))
            v.tensor_tensor(hot_src[:, :, :].rearrange("p t (a n) -> p t a n", a=2),
                            f_src.unsqueeze(2).unsqueeze(3).to_broadcast([P, ET, 2, N]),
                            iota[:, 0:N].unsqueeze(1).unsqueeze(1).to_broadcast([P, ET, 2, N]),
                            ALU.is_equal).then_inc(hot3_ready, 1)
            v.tensor_tensor(hot3[:, :, :], keys[:, 0, :].unsqueeze(2).to_broadcast([P, ET, R3 * N]),
                            iota[:, 0:R3 * N].unsqueeze(1).to_broadcast([P, ET, R3 * N]),
                            ALU.is_equal).then_inc(hot3_ready, 1)

            def split_block(m):
                h, k = m // (B // 2), m % (B // 2)
                cols = slice(h * HD, (h + 1) * HD)
                dve.wait_ge(qg_high, m + 1)
                hi = high[:, m % 2, :]
                tell(v.tensor_tensor(x_low[:, :], ps_g[:, m % 4, 0:HD], hi, ALU.subtract), qg_read, m + 1)
                if m:
                    dve.wait_ge(qg_placed, 4 * m)
                tell(v.tensor_copy(mid[:, :], x_low[:, :]), qg_mid, m + 1)
                link(v.tensor_tensor(low[:, :], x_low[:, :], mid[:, :], ALU.subtract))
                for hh in range(2):
                    ins = v.tensor_copy(lows(2 * k + hh)[0:N, cols], low[hh * N:(hh + 1) * N, :])
                tell(ins, qg_split, m + 1)

            def one_hot8(half):
                n = (ET + 1 - half) // 2
                t = slice(ET - n, ET) if half else slice(0, n)
                v.tensor_tensor(hot8[:, t, :], keys[:, 1, t].unsqueeze(2).to_broadcast([P, n, R8 * N]),
                                iota.unsqueeze(1).to_broadcast([P, n, R8 * N]), ALU.is_equal).then_inc(hot8_ready, 1)

            def t_copy(turn, to=xt):
                dve.wait_ge(xt_done, 2 * TURNS.index(turn) + 1)
                v.tensor_copy(to[:, 0:LATE * N], early_ps(turn)).then_inc(xt_early, 1)

            split_block(0)
            one_hot8(0)
            dve.wait_ge(const_in, 16)
            dve.wait_ge(counts3, 1)
            tell(v.tensor_copy(raw3, ps_t[:, 0, 0:R3 * N]), a3_copied)
            link(v.tensor_tensor(mask[:, :], raw3[:, 0:N], raw3[:, N:2 * N], ALU.add))
            link(v.tensor_tensor(far[:, :], raw3[:, 2 * N:3 * N], eye, ALU.add))
            tell(v.tensor_tensor(c_sd[:, :, :], mask[:, :].unsqueeze(1).to_broadcast([P, 2, N]),
                                 far[:, :].unsqueeze(1).to_broadcast([P, 2, N]), ALU.add), csd_ready)
            split_block(1)
            dve.wait_ge(cnt3_ps, 1)
            link(v.tensor_scalar(cnt3[:, :], ps_t[:, 1, 0:R3 * N], 1.0, None, ALU.max))
            link(v.reciprocal(cnt3[:, :], cnt3[:, :]))
            for rows, r, to in ((0, 0, 0), (1, 1, 0), (0, 2, 1), (1, 2, 2)):
                half, cols = slice(rows * N, (rows + 1) * N), slice(r * N, (r + 1) * N)
                v.tensor_tensor(a3[half, to, :], raw3[half, cols], cnt3[half, cols], ALU.mult).then_inc(a3_ready, 1)
            dve.wait_ge(cds_ps, 1)
            link(v.tensor_copy(c_ds[:, :], ps_x[:, 0:N]))
            link(v.tensor_reduce(deg[:, :], c_ds[:, :], AX.X, ALU.add))
            v.tensor_copy(dinv_row[:, :], ps_x[:, N:2 * N]).then_inc(deg_ready, 1)
            split_block(2)
            one_hot8(1)
            for m in range(3, B):
                if m == B - 1:
                    dve.wait_ge(counts8, 1)
                    tell(v.tensor_copy(a8[:, :], ps_t[:, 0, :]), a8_copied)
                    t_copy("rgcn1")
                split_block(m)

            def rest_of_adjacency():
                dve.wait_ge(cnt8_ps, 1)
                link(v.tensor_scalar(cnt8[:, :], ps_acc[:, :], 1.0, None, ALU.max))
                link(v.reciprocal(cnt8[:, :], cnt8[:, :]))
                by_pair = [m[half * N:(half + 1) * N, :].rearrange("p (q r n) -> p q r n", q=R8 // 2, r=2)
                           for half in range(2) for m in (a8, cnt8)]
                for half in range(2):
                    m, scale = by_pair[2 * half:2 * half + 2]
                    v.tensor_tensor(m[:, :, 0, :], m[:, :, half, :], scale[:, :, half, :], ALU.mult).then_inc(a8_ready, 1)
                dve.wait_ge(dinv_ready, 2)
                dve.wait_ge(zeros_set, 1)
                for h in range(2):
                    r = slice(h * N, (h + 1) * N)
                    link(v.scalar_tensor_tensor(out=al_t[r, h, :], in0=c_sd[r, 0, :], scalar=dinv_col[r, :], in1=dinv_row[r, :],
                                                op0=ALU.mult, op1=ALU.mult))
                link(v.tensor_scalar(mask[:, :], c_ds[:, :], 0.0, None, ALU.is_gt))
                link(v.tensor_scalar(far[:, :], mask[:, :], 1.0, -FAR, ALU.subtract, ALU.mult))

            def y_copy(name, rels):
                for p in range((rels + 1) // 2):
                    if p < rels // 2:
                        dve.wait_ge(y_done[name], p + 1)
                    else:
                        dve.wait_ge(used, first_load[name] + rels)
                    if p >= 2:
                        dve.wait_ge(y_used[name], p - 1)
                    dst, src = y_s[:, p % 2, 0, :], ps_g[:, 2 * (p % 2), 0:HD]
                    if name == "r8a":
                        v.tensor_scalar(dst, src, st[:, 4:5], None, ALU.mult).then_inc(y_v[name], 1)
                    else:
                        v.tensor_copy(dst, src).then_inc(y_v[name], 1)
                    if name == "r8a" and p == 1:
                        t_copy("r8a_x", qit)

            def relu(name, done, src):
                if name in gats:
                    dve.wait_ge(mix_done[name], 1)
                elif name in relational:
                    dve.wait_ge(summed[name], 1)
                elif name == "gcn1":
                    dve.wait_ge(gcn_summed, 1)
                else:
                    dve.wait_ge(used, last_of(name))
                for cols in (FIRST, LAST):
                    v.tensor_scalar(xs["a"][:, cols], src[:, cols], 0.0, None, ALU.max).then_inc(done, 1)

            def gate(g):
                h = xs["a"]
                t_copy(f"{g}_h")
                dve.wait_ge(used, last_of(f"hg_{g}"))
                dve.wait_ge(hg_high[g], 1)
                link(v.tensor_tensor(x_low[:, :], acc, high[:, 0, :], ALU.subtract))
                tell(v.tensor_copy(mid[:, :], x_low[:, :]), hg_split[g], 1)
                v.tensor_tensor(low[:, :], x_low[:, :], mid[:, :], ALU.subtract).then_inc(hg_split[g], 1)
                for b in range(0, B, 2):
                    dve.wait_ge(gathered[g], b // 4 + 1)
                    v.tensor_copy(*gathered_rows(b)).then_inc(rows_v[g], 1)
                dve.wait_ge(query_doubled, GATE_SLOTS)

                def gate_sums(group):
                    dve.wait_ge(tile_red[g], (group + 1) * TILES // 2)
                    for part in range(2):
                        v.tensor_copy(*qi_quarter(0, group, part)).then_inc(qi_v[g], 1)

                for t in range(TILES):
                    b = t // Q_TILES
                    if t == TILES // 2 + 3:
                        gate_sums(0)
                    dve.wait_ge(tile_sig[g], t + 1)
                    if t >= 2:
                        dve.wait_ge(tile_red[g], t - 1)
                    v.tensor_tensor(prod[:, t % 2, :], att_s[:, t % 2, :], q_rows(b), ALU.mult).then_inc(tile_prod[g], 1)
                gate_sums(1)
                t_copy(f"{g}_q", qit)
                dve.wait_ge(tanh_done[g], 1)
                link(v.tensor_tensor(th[:, :], th[:, :], h[:, :], ALU.subtract))
                if g == "g2":
                    link(v.tensor_tensor(xs["a"][:, :], xs["a"][:, :], xs["in"][:, :], ALU.add))
                for i, cols in enumerate((FIRST, LAST)):
                    dve.wait_ge(al_done[g], i + 1)
                    link(v.tensor_tensor(alpha[:, cols], alpha[:, cols], th[:, cols], ALU.mult))
                    if g == "g1":
                        v.tensor_tensor(xs["b"][:, cols], alpha[:, cols], xs["a"][:, cols], ALU.add).then_inc(state["rgcn2"], 1)

            def center(n, other, res, done):
                y = xs["y"]
                tell(v.tensor_tensor_reduce(y[:, :], other, res, 1.0, 0.0, ALU.add, ALU.add, st[:, 0:1]), sum_ready, n + 1)
                dve.wait_ge(mean_ps, n + 1)
                for cols in (FIRST, LAST):
                    v.tensor_scalar(y[:, cols], y[:, cols], ps_s[:, 0:1], None, ALU.subtract).then_inc(done, 1)

            def scale(n, centered):
                y = xs["y"]
                dve.wait_ge(centered, 2)
                v.tensor_tensor_reduce(x_low[:, :], y[:, :], y[:, :], 1.0, 0.0, ALU.mult, ALU.add, st[:, 1:2]).then_inc(square_ready, 1)
                dve.wait_ge(square_ps, n + 1)
                v.tensor_scalar(st[:, 3:4], ps_s[:, 1:2], EPS, None, ALU.add).then_inc(var_ready, 1)
                dve.wait_ge(rstd_ready, n + 1)
                tell(v.tensor_scalar(xs["in"][:, :], y[:, :], st[:, 4:5], None, ALU.mult), x_ready, n + 1)

            def last_norm():
                link(v.bn_stats(stat[:, :], acc))
                v.bn_aggr(mv[:, :], stat[:, :]).then_inc(mv_ready, 1)
                dve.wait_ge(mv_ps, 1)
                link(v.tensor_scalar(st[:, 5:6], ps_s[:, 1:2], EPS, None, ALU.add))
                v.scalar_tensor_tensor(out=st[:, 3:4], in0=ps_s[:, 2:3], scalar=ps_s[:, 2:3], in1=st[:, 5:6],
                                       op0=ALU.mult, op1=ALU.add).then_inc(var_ready, 1)
                dve.wait_ge(rstd_ready, 4)
                v.tensor_scalar(xs["y"][:, :], acc, ps_s[:, 0:1], st[:, 4:5], ALU.subtract, ALU.mult).then_inc(result, 1)

            rest_of_adjacency()
            y_copy("rgcn1", R3)
            relu("rgcn1", h_ready["g1"], acc2)
            gate("g1")
            t_copy("rgcn2")
            y_copy("rgcn2", R3)
            relu("rgcn2", h_ready["g2"], acc2)
            gate("g2")
            center(0, alpha[:, :], xs["a"][:, :], state["gcn1"])
            t_copy("gcn1")
            scale(0, state["gcn1"])
            dve.wait_ge(used, last_of("gcn1"))
            v.tensor_scalar(y_s[:, 0, 0, :], acc, st[:, 4:5], None, ALU.mult).then_inc(gcn_copied, 1)
            relu("gcn1", state["gcn2"], acc2)
            t_copy("gcn2")
            dve.wait_ge(used, last_of("gcn2"))
            center(1, acc, xs["in"][:, :], state["gat1"])
            dve.wait_ge(att_in, 16 * 8)
            for k, name in enumerate(gats):
                t_copy(name)
                if k == 0:
                    scale(1, state["gat1"])
                dve.wait_ge(used, last_of(name))
                for a in range(2):
                    v.tensor_tensor_reduce(x_low[:, :], acc2, att_rows[:, 2 * k + a, :], 1.0, 0.0,
                                           ALU.mult, ALU.add, a_part[:, a:a + 1]).then_inc(terms[name], 1)
                    dve.wait_ge(terms[name], a + 1)
                    if k == 0 and a == 0:
                        v.tensor_scalar(diag[:, :], eye, a_part[:, 0:1], st[:, 4:5], ALU.mult, ALU.mult).then_inc(diag_ready[name], 1)
                    elif a == 0:
                        v.tensor_scalar(diag[:, :], eye, a_part[:, 0:1], None, ALU.mult).then_inc(diag_ready[name], 1)
                    elif k == 0:
                        v.tensor_scalar(st[:, 6:7], a_part[:, 1:2], st[:, 4:5], None, ALU.mult).then_inc(terms[name], 1)
                if k == 0:
                    v.tensor_scalar(qi[:, :], acc2, st[:, 4:5], None, ALU.mult).then_inc(h_copied[name], 1)
                else:
                    v.tensor_copy(qi[:, :], acc2).then_inc(h_copied[name], 1)
                dve.wait_ge(logits_ps[name], 1)
                link(v.tensor_scalar(e_t[:, 0, :], ps_s[:, 0:N], ps_s[:, N:N + 1], -1.0, ALU.add, ALU.mult))
                link(v.scalar_tensor_tensor(out=e_t[:, 2, :], in0=e_t[:, 0, :], scalar=SLOPE, in1=e_t[:, 0, :],
                                            op0=ALU.mult, op1=ALU.min))
                v.tensor_tensor_reduce(e_t[:, 0, :], e_t[:, 2, :], far[:, :], 1.0, FAR,
                                       ALU.add, ALU.min, st[:, 7:8]).then_inc(exp_in[name], 1)
                dve.wait_ge(exp_done[name], 1)
                link(v.tensor_tensor_reduce(e_t[:, 2, :], e_t[:, 1, :], c_ds[:, :], 1.0, 0.0, ALU.mult, ALU.add, st[:, 5:6]))
                link(v.reciprocal(st[:, 6:7], st[:, 5:6]))
                v.tensor_scalar(e_t[:, 3:5, :], e_t[:, 2, :].unsqueeze(1).to_broadcast([P, 2, N]), st[:, 6:7], None, ALU.mult).then_inc(alpha_ready[name], 1)
                dve.wait_ge(alphat_ps[name], 1)
                v.tensor_copy(al_t[0:N, 0, :], ps_x[0:N, 0:N]).then_inc(alphat_ready[name], 1)
                if k == 0:
                    relu(name, state["gat2"], acc)
            dve.wait_ge(mix_done["gat2"], 1)
            center(2, acc, xs["in"][:, :], state["r8a"])
            t_copy("r8a")
            scale(2, state["r8a"])
            y_copy("r8a", R8)
            relu("r8a", state["r8b"], acc2)
            t_copy("r8b")
            y_copy("r8b", R8)
            dve.wait_ge(summed["r8b"], 1)
            last_norm()


def kernel(**inputs):
    import concourse.bacc as bacc
    from concourse.bass_utils import run_bass_kernel_spmd

    get = {k: np.asarray(v) for k, v in inputs.items()}

    def chunked(w):
        return w.reshape(KC, P, -1).transpose(1, 0, 2).reshape(P, -1)

    mats = {"root1": get["L0_gnn_W_root1"], "root2": get["L0_gnn_W_root2"],
            "Wg_h": get["L0_gnn_Wg"][:, :D].T, "Wg_q": get["L0_gnn_Wg"][:, D:].T,
            "Wq_h": get["L0_gnn_Wq"][:, :D].T, "Wq_q": get["L0_gnn_Wq"][:, D:].T,
            "gcn1": get["L1_gnn_W1"], "gcn2": get["L1_gnn_W2"], "gat1": get["L2_gnn_W1"], "gat2": get["L2_gnn_W2"],
            "r8a_root": get["L3_gnn_root1"], "r8b_root": get["L3_gnn_root2"]}
    for r in range(R3):
        mats[f"rel1_{r}"], mats[f"rel2_{r}"] = get["L0_gnn_W_rel1"][r], get["L0_gnn_W_rel2"][r]
    for r in range(R8):
        mats[f"r8a_{r}"], mats[f"r8b_{r}"] = get["L3_gnn_W1"][r], get["L3_gnn_W2"][r]
    query = get["L0_gnn_query_embs"]
    biases = [get[k.replace("_", "_gnn_")] for k in BIAS]
    att = [get[k] for k in ("L2_gnn_att_src1", "L2_gnn_att_dst1", "L2_gnn_att_src2", "L2_gnn_att_dst2")]
    edges = np.stack([get[k] for k in ("src", "dst", "edge_type_3", "edge_type_8")])
    arrays = {
        "x": get["x"],
        "edges": edges[:, :FULL * P].reshape(4, P, FULL).transpose(1, 0, 2),
        "edges_rest": edges[:, FULL * P:].T,
        "consts": constants(),
        "consts16": bf16_constants(),
        "picks": bias_picks(),
        "biases": np.stack(biases),
        "query_t": query.reshape(B // 2, P, KC, P).transpose(3, 0, 2, 1).reshape(P, -1),
        "query": np.ascontiguousarray(query.transpose(1, 0, 2)),
        "att": np.stack(att),
        "weights": np.stack([chunked(mats[n]) for n in NAMES]),
    }
    arrays = {k: np.ascontiguousarray(v) for k, v in arrays.items()}
    nc = bacc.Bacc("TRN2", target_bir_lowering=False, num_devices=1)
    args = [nc.dram_tensor(f"in_{k}", a.shape, mybir.dt.from_np(a.dtype), kind="ExternalInput").ap() for k, a in arrays.items()]
    out = nc.dram_tensor("out", (N, D), F32, kind="ExternalOutput").ap()
    build(nc, *args, out)
    r = run_bass_kernel_spmd(nc, [{f"in_{k}": a for k, a in arrays.items()}], core_ids=[0])
    return r.results[0]["out"]
```
